# Optimizing a Trainium2 kernel written in Bass

```python
import numpy as np
import jax
import jax.numpy as jnp

def _softmax(x, axis=-1):
    return jax.nn.softmax(x, axis=axis)

def _gelu(x):
    return jax.nn.gelu(x, approximate=True)

def _silu(x):
    return jax.nn.silu(x)

def _sigmoid(x):
    return jax.nn.sigmoid(x)

def _layernorm(x, axis=-1, eps=1e-05):
    m = jnp.mean(x, axis=axis, keepdims=True)
    v = jnp.var(x, axis=axis, keepdims=True)
    return (x - m) / jnp.sqrt(v + eps)

def _scatter_add(tgt, idx, src, axis=0):
    return tgt.at[idx].add(src)

def _segment_sum(src, seg, n):
    return jax.ops.segment_sum(src, seg, n)
kernel_name = 'mk_gnn_resnorm_d4_gnn_r32_586bf6'

def setup_inputs(seed: int=0):
    np.random.seed(seed)
    _w = jnp.asarray

    def _rec_inputs():
        import jax
        import jax.numpy as jnp
        _gk = jax.random.key(seed)
        x = -0.0003713 + 1 * jax.random.normal(jax.random.fold_in(_gk, 1), (3125, 128), jnp.float32)
        _s = jax.random.randint(jax.random.fold_in(_gk, 2), (25000,), 0, 3125, jnp.int32)
        _d = jax.random.randint(jax.random.fold_in(_gk, 3), (25000,), 0, 3125, jnp.int32)
        _loop = jnp.arange(3125, dtype=jnp.int32)
        src = jnp.concatenate([_s, _d, _loop])
        dst = jnp.concatenate([_d, _s, _loop])
        _o = jnp.argsort(dst, stable=True)
        src = src[_o]
        dst = dst[_o]
        edge_attr_128 = -4.21973e-05 + 0.999841 * jax.random.normal(jax.random.fold_in(_gk, 12), (53125, 128), jnp.float32)
        return (x, src, dst, edge_attr_128)
    x, src, dst, edge_attr_128 = _rec_inputs()

    def _L0_gnn_setup():
        import jax, jax.numpy as jnp
        import numpy as np
        N = 3125
        E = 50000
        IN = 128
        HID = 128
        BN_EPS = 1e-05

        def _mlp_bn(h, w_a, b_a, g, bt, w_b, b_b):
            h = h @ w_a + b_a
            mu = h.mean(axis=0)
            var = h.var(axis=0)
            h = (h - mu) * jax.lax.rsqrt(var + BN_EPS) * g + bt
            h = jax.nn.relu(h)
            return h @ w_b + b_b

        def _gin(x, src, dst, eps, w_a, b_a, g, bt, w_b, b_b):
            agg = jax.ops.segment_sum(x[src], dst, num_segments=N)
            return _mlp_bn((1.0 + eps) * x + agg, w_a, b_a, g, bt, w_b, b_b)
        key = jax.random.key(seed)
        ks = jax.random.split(key, 8)

        def glorot(k, shape):
            lim = np.sqrt(6.0 / (shape[0] + shape[1])).astype(np.float32)
            return jax.random.uniform(k, shape, minval=-lim, maxval=lim, dtype=jnp.float32)
        return {'x': jax.random.normal(ks[0], (N, IN), dtype=jnp.float32), 'src': jax.random.randint(ks[1], (E,), 0, N), 'dst': jax.random.randint(ks[2], (E,), 0, N), 'eps1': jnp.float32(0.1), 'w1a': glorot(ks[3], (IN, HID)), 'b1a': jnp.zeros((HID,), jnp.float32), 'g1': jnp.ones((HID,), jnp.float32), 'bt1': jnp.zeros((HID,), jnp.float32), 'w1b': glorot(ks[4], (HID, HID)), 'b1b': jnp.zeros((HID,), jnp.float32), 'eps2': jnp.float32(0.1), 'w2a': glorot(ks[5], (HID, HID)), 'b2a': jnp.zeros((HID,), jnp.float32), 'g2': jnp.ones((HID,), jnp.float32), 'bt2': jnp.zeros((HID,), jnp.float32), 'w2b': glorot(ks[6], (HID, HID)), 'b2b': jnp.zeros((HID,), jnp.float32)}
    _L0_gnn_all = _L0_gnn_setup()
    _L0_gnn_in = {k: v for k, v in _L0_gnn_all.items() if k in ('eps1', 'w1a', 'b1a', 'g1', 'bt1', 'w1b', 'b1b', 'eps2', 'w2a', 'b2a', 'g2', 'bt2', 'w2b', 'b2b')}
    del _L0_gnn_all

    def _L1_gnn_setup():
        import jax, jax.numpy as jnp
        import numpy as np
        HIDDEN = 128
        N_NODES = 50000
        N_EDGES = 18750
        EPS = 1e-05

        def _linear_params(key, fan_in, fan_out):
            kw, kb = jax.random.split(key)
            bound = 1.0 / np.sqrt(fan_in)
            W = jax.random.uniform(kw, (fan_in, fan_out), jnp.float32, -bound, bound)
            b = jax.random.uniform(kb, (fan_out,), jnp.float32, -bound, bound)
            return (W, b)

        def _mlp2(x, W1, b1, W2, b2):
            h = jax.nn.silu(x @ W1 + b1)
            return h @ W2 + b2

        def _layernorm(x, gamma, beta):
            mu = jnp.mean(x, axis=-1, keepdims=True)
            var = jnp.mean(jnp.square(x - mu), axis=-1, keepdims=True)
            return (x - mu) * jax.lax.rsqrt(var + EPS) * gamma + beta
        key = jax.random.key(seed)
        ks = jax.random.split(key, 8)
        h_node = jax.random.normal(ks[0], (N_NODES, HIDDEN), jnp.float32)
        h_edge = jax.random.normal(ks[1], (N_EDGES, HIDDEN), jnp.float32)
        edge_index = jax.random.randint(ks[2], (2, N_EDGES), 0, N_NODES, jnp.int64 if jax.config.jax_enable_x64 else jnp.int32)
        msg_W1, msg_b1 = _linear_params(ks[3], 3 * HIDDEN, HIDDEN)
        msg_W2, msg_b2 = _linear_params(ks[4], HIDDEN, HIDDEN)
        upd_W1, upd_b1 = _linear_params(ks[5], 2 * HIDDEN, HIDDEN)
        upd_W2, upd_b2 = _linear_params(ks[6], HIDDEN, HIDDEN)
        ln_gamma = jnp.ones((HIDDEN,), jnp.float32)
        ln_beta = jnp.zeros((HIDDEN,), jnp.float32)
        return {'h_node': h_node, 'h_edge': h_edge, 'edge_index': edge_index, 'msg_W1': msg_W1, 'msg_b1': msg_b1, 'msg_W2': msg_W2, 'msg_b2': msg_b2, 'upd_W1': upd_W1, 'upd_b1': upd_b1, 'upd_W2': upd_W2, 'upd_b2': upd_b2, 'ln_gamma': ln_gamma, 'ln_beta': ln_beta}
    _L1_gnn_all = _L1_gnn_setup()
    _L1_gnn_in = {k: v for k, v in _L1_gnn_all.items() if k in ('msg_W1', 'msg_b1', 'msg_W2', 'msg_b2', 'upd_W1', 'upd_b1', 'upd_W2', 'upd_b2', 'ln_gamma', 'ln_beta')}
    del _L1_gnn_all

    def _L2_gnn_setup():
        import jax, jax.numpy as jnp
        import numpy as np
        N_NODES = 1250
        N_EDGES = 20000
        D = 128
        EMB = 2 * D
        L = 3
        BN_EPS = 1e-05

        def _gin_forward(h, e, W1, b1, gamma, beta, W2, b2, src, dst):
            n_layers = W1.shape[0]
            n_nodes = h.shape[0]
            for l in range(n_layers):
                x = jnp.concatenate([h[src], e], axis=1)
                x = x @ W1[l].T + b1[l]
                mu = jnp.mean(x, axis=0)
                var = jnp.var(x, axis=0)
                x = (x - mu) * jax.lax.rsqrt(var + BN_EPS) * gamma[l] + beta[l]
                x = jax.nn.relu(x)
                m = x @ W2[l].T + b2[l]
                h = jax.ops.segment_sum(m, dst, num_segments=n_nodes)
                if l < n_layers - 1:
                    h = jax.nn.relu(h)
                    e = jax.nn.relu(e)
            return h
        key = jax.random.key(seed)
        ks = jax.random.split(key, 8)
        h = jax.random.normal(ks[0], (N_NODES, D), jnp.float32)
        e = jax.random.normal(ks[1], (N_EDGES, D), jnp.float32)
        src = jax.random.randint(ks[2], (N_EDGES,), 0, N_NODES, dtype=jnp.int32)
        dst = jax.random.randint(ks[3], (N_EDGES,), 0, N_NODES, dtype=jnp.int32)
        s = 1.0 / np.sqrt(EMB)
        W1 = jax.random.normal(ks[4], (L, EMB, EMB), jnp.float32) * s
        b1 = jnp.zeros((L, EMB), jnp.float32)
        gamma = jnp.ones((L, EMB), jnp.float32)
        beta = jnp.zeros((L, EMB), jnp.float32)
        W2 = jax.random.normal(ks[5], (L, D, EMB), jnp.float32) * s
        b2 = jnp.zeros((L, D), jnp.float32)
        return {'h': h, 'e': e, 'W1': W1, 'b1': b1, 'gamma': gamma, 'beta': beta, 'W2': W2, 'b2': b2, 'src': src, 'dst': dst}
    _L2_gnn_all = _L2_gnn_setup()
    _L2_gnn_in = {k: v for k, v in _L2_gnn_all.items() if k in ('W1', 'b1', 'gamma', 'beta', 'W2', 'b2')}
    del _L2_gnn_all

    def _L3_gnn_setup():
        import jax, jax.numpy as jnp
        import numpy as np
        N_NODES = 3125
        N_EDGES = 50000
        D = 128

        def _sage_layer(x, src, dst, W, b):
            msgs = x[src]
            agg = jax.ops.segment_sum(msgs, dst, num_segments=N_NODES)
            return agg @ W.T + b
        key = jax.random.key(seed)
        k_x, k_e, k_w1, k_w2 = jax.random.split(key, 4)
        x = jax.random.normal(k_x, (N_NODES, D), dtype=jnp.float32)
        edge_index = jax.random.randint(k_e, (2, N_EDGES), 0, N_NODES, dtype=jnp.int64)
        W1 = jax.random.normal(k_w1, (D, D), dtype=jnp.float32) * 0.05
        b1 = jnp.zeros((D,), dtype=jnp.float32)
        W2 = jax.random.normal(k_w2, (D, D), dtype=jnp.float32) * 0.05
        b2 = jnp.zeros((D,), dtype=jnp.float32)
        return {'x': x, 'edge_index': edge_index, 'W1': W1, 'b1': b1, 'W2': W2, 'b2': b2}
    _L3_gnn_all = _L3_gnn_setup()
    _L3_gnn_in = {k: v for k, v in _L3_gnn_all.items() if k in ('W1', 'b1', 'W2', 'b2')}
    del _L3_gnn_all
    return {'x': x, 'src': src, 'dst': dst, 'edge_attr_128': edge_attr_128, 'L0_gnn_eps1': _L0_gnn_in['eps1'], 'L0_gnn_w1a': _L0_gnn_in['w1a'], 'L0_gnn_b1a': _L0_gnn_in['b1a'], 'L0_gnn_g1': _L0_gnn_in['g1'], 'L0_gnn_bt1': _L0_gnn_in['bt1'], 'L0_gnn_w1b': _L0_gnn_in['w1b'], 'L0_gnn_b1b': _L0_gnn_in['b1b'], 'L0_gnn_eps2': _L0_gnn_in['eps2'], 'L0_gnn_w2a': _L0_gnn_in['w2a'], 'L0_gnn_b2a': _L0_gnn_in['b2a'], 'L0_gnn_g2': _L0_gnn_in['g2'], 'L0_gnn_bt2': _L0_gnn_in['bt2'], 'L0_gnn_w2b': _L0_gnn_in['w2b'], 'L0_gnn_b2b': _L0_gnn_in['b2b'], 'L1_gnn_msg_W1': _L1_gnn_in['msg_W1'], 'L1_gnn_msg_b1': _L1_gnn_in['msg_b1'], 'L1_gnn_msg_W2': _L1_gnn_in['msg_W2'], 'L1_gnn_msg_b2': _L1_gnn_in['msg_b2'], 'L1_gnn_upd_W1': _L1_gnn_in['upd_W1'], 'L1_gnn_upd_b1': _L1_gnn_in['upd_b1'], 'L1_gnn_upd_W2': _L1_gnn_in['upd_W2'], 'L1_gnn_upd_b2': _L1_gnn_in['upd_b2'], 'L1_gnn_ln_gamma': _L1_gnn_in['ln_gamma'], 'L1_gnn_ln_beta': _L1_gnn_in['ln_beta'], 'L2_gnn_W1': _L2_gnn_in['W1'], 'L2_gnn_b1': _L2_gnn_in['b1'], 'L2_gnn_gamma': _L2_gnn_in['gamma'], 'L2_gnn_beta': _L2_gnn_in['beta'], 'L2_gnn_W2': _L2_gnn_in['W2'], 'L2_gnn_b2': _L2_gnn_in['b2'], 'L3_gnn_W1': _L3_gnn_in['W1'], 'L3_gnn_b1': _L3_gnn_in['b1'], 'L3_gnn_W2': _L3_gnn_in['W2'], 'L3_gnn_b2': _L3_gnn_in['b2']}

def reference(x, src, dst, edge_attr_128, L0_gnn_eps1, L0_gnn_w1a, L0_gnn_b1a, L0_gnn_g1, L0_gnn_bt1, L0_gnn_w1b, L0_gnn_b1b, L0_gnn_eps2, L0_gnn_w2a, L0_gnn_b2a, L0_gnn_g2, L0_gnn_bt2, L0_gnn_w2b, L0_gnn_b2b, L1_gnn_msg_W1, L1_gnn_msg_b1, L1_gnn_msg_W2, L1_gnn_msg_b2, L1_gnn_upd_W1, L1_gnn_upd_b1, L1_gnn_upd_W2, L1_gnn_upd_b2, L1_gnn_ln_gamma, L1_gnn_ln_beta, L2_gnn_W1, L2_gnn_b1, L2_gnn_gamma, L2_gnn_beta, L2_gnn_W2, L2_gnn_b2, L3_gnn_W1, L3_gnn_b1, L3_gnn_W2, L3_gnn_b2):
    import jax
    import jax.numpy as jnp

    def _L0_gnn_ref(x, src, dst, eps1, w1a, b1a, g1, bt1, w1b, b1b, eps2, w2a, b2a, g2, bt2, w2b, b2b):
        import jax, jax.numpy as jnp
        import numpy as np
        N = 3125
        E = 50000
        IN = 128
        HID = 128
        BN_EPS = 1e-05

        def _mlp_bn(h, w_a, b_a, g, bt, w_b, b_b):
            h = h @ w_a + b_a
            mu = h.mean(axis=0)
            var = h.var(axis=0)
            h = (h - mu) * jax.lax.rsqrt(var + BN_EPS) * g + bt
            h = jax.nn.relu(h)
            return h @ w_b + b_b

        def _gin(x, src, dst, eps, w_a, b_a, g, bt, w_b, b_b):
            agg = jax.ops.segment_sum(x[src], dst, num_segments=N)
            return _mlp_bn((1.0 + eps) * x + agg, w_a, b_a, g, bt, w_b, b_b)
        h = jax.nn.relu(_gin(x, src, dst, eps1, w1a, b1a, g1, bt1, w1b, b1b))
        h = _gin(h, src, dst, eps2, w2a, b2a, g2, bt2, w2b, b2b)
        return h

    def _L1_gnn_ref(h_node, h_edge, edge_index, msg_W1, msg_b1, msg_W2, msg_b2, upd_W1, upd_b1, upd_W2, upd_b2, ln_gamma, ln_beta):
        import jax, jax.numpy as jnp
        import numpy as np
        HIDDEN = 128
        N_NODES = 50000
        N_EDGES = 18750
        EPS = 1e-05

        def _linear_params(key, fan_in, fan_out):
            kw, kb = jax.random.split(key)
            bound = 1.0 / np.sqrt(fan_in)
            W = jax.random.uniform(kw, (fan_in, fan_out), jnp.float32, -bound, bound)
            b = jax.random.uniform(kb, (fan_out,), jnp.float32, -bound, bound)
            return (W, b)

        def _mlp2(x, W1, b1, W2, b2):
            h = jax.nn.silu(x @ W1 + b1)
            return h @ W2 + b2

        def _layernorm(x, gamma, beta):
            mu = jnp.mean(x, axis=-1, keepdims=True)
            var = jnp.mean(jnp.square(x - mu), axis=-1, keepdims=True)
            return (x - mu) * jax.lax.rsqrt(var + EPS) * gamma + beta
        src, dst = (edge_index[0], edge_index[1])
        m_in = jnp.concatenate([h_node[src], h_node[dst], h_edge], axis=-1)
        m = _mlp2(m_in, msg_W1, msg_b1, msg_W2, msg_b2)
        agg = jax.ops.segment_sum(m, dst, num_segments=h_node.shape[0])
        h_new = _mlp2(jnp.concatenate([h_node, agg], axis=-1), upd_W1, upd_b1, upd_W2, upd_b2)
        return _layernorm(h_node + h_new, ln_gamma, ln_beta)

    def _L2_gnn_ref(h, e, W1, b1, gamma, beta, W2, b2, src, dst):
        import jax, jax.numpy as jnp
        import numpy as np
        N_NODES = 1250
        N_EDGES = 20000
        D = 128
        EMB = 2 * D
        L = 3
        BN_EPS = 1e-05

        def _gin_forward(h, e, W1, b1, gamma, beta, W2, b2, src, dst):
            n_layers = W1.shape[0]
            n_nodes = h.shape[0]
            for l in range(n_layers):
                x = jnp.concatenate([h[src], e], axis=1)
                x = x @ W1[l].T + b1[l]
                mu = jnp.mean(x, axis=0)
                var = jnp.var(x, axis=0)
                x = (x - mu) * jax.lax.rsqrt(var + BN_EPS) * gamma[l] + beta[l]
                x = jax.nn.relu(x)
                m = x @ W2[l].T + b2[l]
                h = jax.ops.segment_sum(m, dst, num_segments=n_nodes)
                if l < n_layers - 1:
                    h = jax.nn.relu(h)
                    e = jax.nn.relu(e)
            return h
        return _gin_forward(h, e, W1, b1, gamma, beta, W2, b2, src, dst)

    def _L3_gnn_ref(x, edge_index, W1, b1, W2, b2):
        import jax, jax.numpy as jnp
        import numpy as np
        N_NODES = 3125
        N_EDGES = 50000
        D = 128

        def _sage_layer(x, src, dst, W, b):
            msgs = x[src]
            agg = jax.ops.segment_sum(msgs, dst, num_segments=N_NODES)
            return agg @ W.T + b
        src, dst = (edge_index[0], edge_index[1])
        x = jax.nn.relu(_sage_layer(x, src, dst, W1, b1))
        x = jax.nn.relu(_sage_layer(x, src, dst, W2, b2))
        return x
    edge_index = jnp.stack([src, dst])
    x = _layernorm(x + _L0_gnn_ref(x, src, dst, L0_gnn_eps1, L0_gnn_w1a, L0_gnn_b1a, L0_gnn_g1, L0_gnn_bt1, L0_gnn_w1b, L0_gnn_b1b, L0_gnn_eps2, L0_gnn_w2a, L0_gnn_b2a, L0_gnn_g2, L0_gnn_bt2, L0_gnn_w2b, L0_gnn_b2b), axis=-1)
    x = _layernorm(x + _L1_gnn_ref(x, edge_attr_128, edge_index, L1_gnn_msg_W1, L1_gnn_msg_b1, L1_gnn_msg_W2, L1_gnn_msg_b2, L1_gnn_upd_W1, L1_gnn_upd_b1, L1_gnn_upd_W2, L1_gnn_upd_b2, L1_gnn_ln_gamma, L1_gnn_ln_beta), axis=-1)
    x = _layernorm(x + _L2_gnn_ref(x, edge_attr_128, L2_gnn_W1, L2_gnn_b1, L2_gnn_gamma, L2_gnn_beta, L2_gnn_W2, L2_gnn_b2, src, dst), axis=-1)
    x = _layernorm(x + _L3_gnn_ref(x, edge_index, L3_gnn_W1, L3_gnn_b1, L3_gnn_W2, L3_gnn_b2), axis=-1)
    return x

_drawn_inputs = setup_inputs


def setup_inputs(seed=0):
    import zlib

    import numpy as np

    out = dict(_drawn_inputs(seed))
    spreads = {'L0_gnn_b1a': (0.0, 2.0),
     'L0_gnn_g1': (1.0, 0.6),
     'L0_gnn_bt1': (0.0, 0.8),
     'L0_gnn_b1b': (0.0, 0.8),
     'L0_gnn_b2a': (0.0, 2.0),
     'L0_gnn_g2': (1.0, 0.6),
     'L0_gnn_bt2': (0.0, 0.765),
     'L0_gnn_b2b': (0.0, 0.435),
     'L1_gnn_ln_gamma': (1.0, 0.6),
     'L1_gnn_ln_beta': (0.0, 0.8),
     'L2_gnn_b1': (0.0, 2.0),
     'L2_gnn_gamma': (1.0, 0.2),
     'L2_gnn_beta': (0.0, 0.1),
     'L2_gnn_b2': (0.0, 0.1),
     'L3_gnn_b1': (0.0, 0.525),
     'L3_gnn_b2': (0.0, 2.0)}
    factors = {'L1_gnn_msg_W1': 3.132,
     'L1_gnn_msg_b1': 28.238,
     'L1_gnn_msg_W2': 2.789,
     'L1_gnn_msg_b2': 18.38,
     'L1_gnn_upd_b1': 64.0,
     'L1_gnn_upd_b2': 31.752}
    for name, (base, spread) in spreads.items():
        noise = np.random.default_rng([zlib.crc32(name.encode()), seed]).standard_normal(out[name].shape)
        drawn = base * np.exp(spread * noise) if base else spread * noise
        out[name] = jnp.asarray(drawn.astype(out[name].dtype))
    for name, factor in factors.items():
        out[name] = (out[name] * factor).astype(out[name].dtype)
    return out
```

```python
from contextlib import ExitStack

import concourse.bass as bass
from concourse import mybir

F32 = mybir.dt.float32
I32 = mybir.dt.int32
ALU = mybir.AluOpType
ACT = mybir.ActivationFunctionType
AX = mybir.AxisListType

D = 128
N_NODES = 3125
N_TILES = -(-N_NODES // D)
NP = N_TILES * D
N_EDGES = 53125
GC = 4
GE = GC * D
NG = -(-N_EDGES // GE)
EP = NG * GE
WIN = 64
N_WIN = NP // WIN
UNROLL = 4
EPS = 1e-5
TINY = 1e-30
N_LAYERS2 = 3

WEIGHTS, _at = {}, 0
for _n, _w in ([("w1a", 1), ("w1b", 1), ("w2a", 1), ("w2b", 1), ("msg_xs", 1), ("msg_xd", 1), ("msg_e", 1),
                ("msg_2", 1), ("upd_x", 1), ("upd_a", 1), ("upd_2", 1), ("sage1", 1), ("sage2", 1)]
               + [(f"{k}{l}", w) for l in range(N_LAYERS2) for k, w in
                  (("eh", 2), ("ee", 2), ("eo_lo", 1), ("eo_hi", 1))]):
    WEIGHTS[_n] = (_at, _w * D)
    _at += _w * D
W_COLS = _at
COLS = ["b1a", "g1", "bt1", "b1b", "b2a", "g2", "bt2", "b2b", "upd_b1", "upd_b2", "sage_b1", "sage_b2"] + [
    f"{k}{l}{h}" for l in range(N_LAYERS2) for k in ("b", "g", "bt") for h in (0, 1)]
ROWS = ["msg_b1", "msg_b2", "ln_g", "ln_b"] + [f"eo_b{l}" for l in range(N_LAYERS2)]


class Count:

    def __init__(self, sem, by=1):
        self.sem, self.by, self.n = sem, by, 0

    def mark(self, ins):
        ins.then_inc(self.sem, self.by)
        self.n += self.by
        return (self.sem, self.n)

    def now(self):
        return (self.sem, self.n)


def wait(eng, *marks):
    for sem, value in marks:
        eng.wait_ge(sem, value)


def hold(eng, *marks):
    for mark in marks:
        wait(eng, mark)
        eng.nop(nofuse=True)


def build(nc, x_n, x_t, e_t, src_g, dst_g, dst_p, weights, cols, rows, eps, out, stop_at=None):
    pe, dve, act, pool, sp = nc.tensor, nc.vector, nc.scalar, nc.gpsimd, nc.sync
    with ExitStack() as ctx:
        def sb(name, shape, dt=F32):
            return ctx.enter_context(nc.sbuf_tensor(name, shape, dt))

        def sem(name):
            return ctx.enter_context(nc.semaphore(name))

        def dram(name, shape):
            return nc.dram_tensor(name, shape, F32, kind="Internal").ap()

        w_all = sb("w_all", [D, W_COLS])
        col_all = sb("col_all", [D, len(COLS)])
        row_all = sb("row_all", [D, len(ROWS) * D])
        eps_sb = sb("eps_sb", [D, 2])
        ident = sb("ident", [D, D])
        ones = sb("ones", [D, D])
        eps_c = sb("eps_c", [D, 1])
        node_no = sb("node_no", [D, NP])
        node_no_i = sb("node_no_i", [D, WIN], I32)
        dst_i = sb("dst_i", [D, NG * GC], I32)
        dst_rel = sb("dst_rel", [D, NG * GC])
        w0_i = sb("w0_i", [1, NG], I32)
        any_wide = sb("any_wide", [1, 1], I32)
        small = sb("small", [D, 64])
        diag = sb("diag", [D, D])
        xT = sb("xT", [D, NP])
        xN = sb("xN", [D, N_TILES, D])
        acc = sb("acc", [D, 2, NP])
        deg = sb("deg", [1, NP])
        tA = sb("tA", [D, NP])
        tN = sb("tN", [D, N_TILES, 2 * D])
        vec = sb("vec", [D, 4 * N_TILES])
        m_ring = sb("m_ring", [D, UNROLL, GC, 2 * D])
        e_ring = sb("e_ring", [D, UNROLL, GE])
        idx_ring = sb("idx_ring", [D, UNROLL, 2, GC], I32)
        oh_ring = sb("oh_ring", [D, 2, GC, WIN])
        oh_wide = sb("oh_wide", [D, GC, WIN])
        sq_ring = sb("sq_ring", [D, 2, GC, 2 * D])
        sgn = sb("sgn", [D, 2 * D])
        low = sb("low", [D, 2 * D])
        v_row = sb("v_row", [1, D])
        chan = sb("chan", [D, 32])

        banks = ctx.enter_context(nc.psum_tensor("banks", [D, 4, 512], F32))
        acc_ps = ctx.enter_context(nc.psum_tensor("acc_ps", [D, 2, 512], F32))
        st_ps = ctx.enter_context(nc.psum_tensor("st_ps", [D, 512], F32))
        x_ps = ctx.enter_context(nc.psum_tensor("x_ps", [D, 512], F32))

        tab0 = dram("tab0", [NP, D])
        tabs = dram("tabs", [NP, D])
        tabd = dram("tabd", [NP, D])
        tab2 = dram("tab2", [NP, 2 * D])
        pre_dram = dram("pre_dram", [NG, D, GC * 2 * D])

        v_done, a_done, p_done, g_done = (Count(sem(s)) for s in ("v_done", "a_done", "p_done", "g_done"))
        loaded = Count(sem("loaded"), 16)
        table_w = Count(sem("table_w"), 16)
        out_w = Count(sem("out_w"), 16)
        idx_in = [Count(sem(f"idx_in{j}"), 16) for j in range(UNROLL)]
        e_in = [Count(sem(f"e_in{j}"), 16) for j in range(UNROLL)]
        rows_in = [Count(sem(f"rows_in{j}"), 16) for j in range(UNROLL)]
        pre_in = [Count(sem(f"pre_in{j}"), 16) for j in range(UNROLL)]
        pre_out = [Count(sem(f"pre_out{j}"), 16) for j in range(UNROLL)]
        e_relu = Count(sem("e_relu"))
        ve_mm = Count(sem("ve_mm"))
        pre = Count(sem("pre"))
        msg = Count(sem("msg"))
        sq = Count(sem("sq"))
        st_mm = Count(sem("st_mm"))
        oh = Count(sem("oh"))
        sc_mm = Count(sem("sc_mm"))
        sc_add = Count(sem("sc_add"))
        oh_x, mm_x, add_x = (Count(sem(s)) for s in ("oh_x", "mm_x", "add_x"))

        def W(name, a=0, b=None):
            at, width = WEIGHTS[name]
            return w_all[:, at + a:at + (width if b is None else b)]

        def col(name):
            i = COLS.index(name)
            return col_all[:, i:i + 1]

        def row(name):
            i = ROWS.index(name)
            return row_all[:, i * D:(i + 1) * D]

        for q, (c, k) in enumerate(((sc_mm, UNROLL), (st_mm, UNROLL), (ve_mm, UNROLL), (pre, 2), (sc_add, 2))):
            pool.memset(small[:, 16 + q:17 + q], 0.0).then_inc(c.sem, k)
            c.n = k
        g_done.mark(pool.memset(small[:, 0:1], 0.0))

        for dst, src in ((w_all[:, :], weights), (col_all[:, :], cols), (dst_i[:, :], dst_p), (xT[:, :], x_t),
                         (row_all[:, :], rows.partition_broadcast(D).rearrange("p a f -> p (a f)")),
                         (eps_sb[:, :], eps.partition_broadcast(D).rearrange("p a f -> p (a f)")),
                         (xN[:, :, :], x_n.rearrange("(t p) f -> p t f", p=D))):
            in_ = loaded.mark(sp.dma_start(dst, src))
        wait(pool, g_done.now())
        g_done.mark(pool.iota(node_no_i[:, :], [[1, WIN]], base=0, channel_multiplier=0))
        g_done.mark(pool.memset(ones[:, :], 1.0))
        g_done.mark(pool.memset(eps_c[:, :], EPS))
        z = g_done.mark(pool.memset(ident[:, :], 0.0))
        wait(pool, z)
        consts = g_done.mark(pool.affine_select(out=ident[:, :], in_=ident[:, :], compare_op=ALU.not_equal, fill=1.0,
                                                base=0, pattern=[[-1, D]], channel_multiplier=1))
        wait(dve, consts)
        t = v_done.mark(dve.tensor_copy(node_no[:, 0:WIN], node_no_i[:, :]))
        for k in range(1, N_WIN):
            wait(dve, t)
            last = v_done.mark(dve.tensor_scalar(node_no[:, k * WIN:(k + 1) * WIN], node_no[:, 0:WIN],
                                                 float(k * WIN), None, ALU.add))
        deg0 = v_done.mark(dve.memset(deg[:, :], 0.0))

        wait(dve, in_)
        t = v_done.mark(dve.tensor_copy(dst_rel[:, :], dst_i[:, :]))
        wait(dve, t)
        big = tA[:, 0:NG * GC]
        t = v_done.mark(dve.tensor_scalar(big, dst_rel[:, :], 0.0, 2.0 * NP, ALU.is_lt, ALU.mult))
        wait(dve, t)
        t = v_done.mark(dve.tensor_tensor(big, big, dst_rel[:, :], ALU.add))
        wait(dve, t)
        gmm = tA[:, 512:512 + 2 * NG]
        v_done.mark(dve.tensor_reduce(gmm[:, 0:NG], big.rearrange("p (g k) -> p g k", k=GC), AX.X, ALU.min))
        t = v_done.mark(dve.tensor_reduce(gmm[:, NG:2 * NG], dst_rel[:, :].rearrange("p (g k) -> p g k", k=GC),
                                          AX.X, ALU.max))
        wait(pe, t, consts)
        for h in range(2):
            t = p_done.mark(pe.transpose(x_ps[0:NG, h * D:(h + 1) * D], gmm[:, h * NG:(h + 1) * NG], ident[:, :]))
        wait(dve, t)
        v_done.mark(dve.tensor_reduce(small[0:NG, 1:2], x_ps[0:NG, 0:D], AX.X, ALU.min))
        t = v_done.mark(dve.tensor_reduce(small[0:NG, 2:3], x_ps[0:NG, D:2 * D], AX.X, ALU.max))
        wait(dve, t)
        t = v_done.mark(dve.tensor_tensor(small[0:NG, 3:4], small[0:NG, 2:3], small[0:NG, 1:2], ALU.subtract))
        wait(dve, t)
        t = v_done.mark(dve.tensor_scalar(small[0:NG, 4:5], small[0:NG, 3:4], float(WIDE_FROM), None, ALU.is_ge))
        wait(pe, t)
        t = p_done.mark(pe.matmul(x_ps[:, 256:257], ones[0:NG, :], small[0:NG, 4:5], start=True, stop=True))
        wait(dve, t)
        v_done.mark(dve.tensor_copy(any_wide[:, :], x_ps[0:1, 256:257]))
        t = v_done.mark(dve.tensor_scalar(small[0:NG, 5:6], x_ps[0:NG, 256:257], 0.0, None, ALU.is_equal))
        wait(dve, t)
        t = v_done.mark(dve.tensor_tensor(small[0:NG, 6:7], small[0:NG, 5:6], small[0:NG, 1:2], ALU.mult))
        wait(dve, t)
        t = v_done.mark(dve.tensor_scalar(diag[0:NG, 0:NG], ident[0:NG, 0:NG], small[0:NG, 6:7], None, ALU.mult))
        wait(pe, t)
        t = p_done.mark(pe.matmul(x_ps[:, 0:NG], ones[0:NG, :], diag[0:NG, 0:NG], start=True, stop=True))
        wait(dve, t)
        v_done.mark(dve.tensor_copy(w0_i[:, :], x_ps[0:1, 0:NG]))
        d3 = dst_rel[:, :].rearrange("p (g k) -> p g k", k=GC)
        windows = v_done.mark(dve.tensor_tensor(d3, d3, x_ps[:, 0:NG].unsqueeze(2).to_broadcast([D, NG, GC]),
                                                ALU.subtract))
        wait(dve, windows)
        wait(pe, windows)
        wide_v = dve.value_load(any_wide[0:1, 0:1], min_val=0, max_val=NG)
        wide_p = pe.value_load(any_wide[0:1, 0:1], min_val=0, max_val=NG)

        def load_idx(g, i, j, srcs, free):
            hold(sp, *free)
            for k, a in enumerate(srcs):
                sp.dma_start(idx_ring[:, j, k, :], a[bass.ds(g, 1), :, :].rearrange("a p k -> (a p) k")
                             ).then_inc(idx_in[j].sem, 16)

        def gather(i, j, tables):
            hold(pool, (idx_in[j].sem, idx_in[j].n + 16 * len(tables) * (i + 1)))
            for k, (table, at, width) in enumerate(tables):
                for c in range(GC):
                    pool.indirect_dma_start(m_ring[:, j, c, at:at + width], None, table[:, :],
                                            bass.IndirectOffsetOnAxis(ap=idx_ring[:, j, k, c:c + 1], axis=0)
                                            ).then_inc(rows_in[j].sem, 16)

        def load_e(g, i, j):
            hold(sp, (ve_mm.sem, ve_mm.n + g - (UNROLL - 1)))
            sp.dma_start(e_ring[:, j, :], e_t[:, bass.ds(g * GE, GE)]).then_inc(e_in[j].sem, 16)

        def one_hot(g, j):
            wait(dve, (sc_mm.sem, sc_mm.n + g - 1))
            dve.tensor_tensor(oh_ring[:, j % 2, :, :], node_no[:, 0:WIN].unsqueeze(1).to_broadcast([D, GC, WIN]),
                              dst_rel[:, bass.ds(g * GC, GC)].unsqueeze(2).to_broadcast([D, GC, WIN]),
                              ALU.is_equal).then_inc(oh.sem, 1)

        def segment_mm(g, j, ready, channels):
            wait(pe, *ready)
            with pe.If(wide_p > 0):
                with pe.Fori(1, N_WIN) as k:
                    at = g * (N_WIN - 1) + k
                    wait(pe, (oh_x.sem, oh_x.n + at))
                    for h, (lhs, m) in enumerate(channels):
                        for c in range(GC):
                            mm = pe.matmul(x_ps[0:m, h * WIN:(h + 1) * WIN], lhs(c), oh_wide[:, c, :],
                                           start=(c == 0), stop=(c == GC - 1))
                    mm.then_inc(mm_x.sem, 1)
            wait(pe, (oh.sem, oh.n + g + 1))
            wait(pe, (sc_add.sem, sc_add.n + g - 1))
            for h, (lhs, m) in enumerate(channels):
                for c in range(GC):
                    mm = pe.matmul(acc_ps[0:m, j % 2, h * WIN:(h + 1) * WIN], lhs(c), oh_ring[:, j % 2, c, :],
                                   start=(c == 0), stop=(c == GC - 1))
            mm.then_inc(sc_mm.sem, 1)

        def segment_add(g, j, sums):
            with dve.If(wide_v > 0):
                with dve.Fori(1, N_WIN) as k:
                    at = g * (N_WIN - 1) + k
                    dve.tensor_tensor(oh_wide[:, :, :],
                                      node_no[:, bass.ds(k * WIN, WIN)].unsqueeze(1).to_broadcast([D, GC, WIN]),
                                      dst_rel[:, bass.ds(g * GC, GC)].unsqueeze(2).to_broadcast([D, GC, WIN]),
                                      ALU.is_equal).then_inc(oh_x.sem, 1)
                    wait(dve, (mm_x.sem, mm_x.n + at))
                    for h, (array, m) in enumerate(sums):
                        a = array[0:m, bass.ds(k * WIN, WIN)]
                        add = dve.tensor_tensor(a, a, x_ps[0:m, h * WIN:(h + 1) * WIN], ALU.add)
                    add.then_inc(add_x.sem, 1)
                    wait(dve, (add_x.sem, add_x.n + at))
            wait(dve, (sc_mm.sem, sc_mm.n + g + 1))
            wait(dve, (sc_add.sem, sc_add.n + g))
            w0 = dve.value_load(w0_i[0:1, bass.ds(g, 1)], min_val=0, max_val=N_NODES - 1)
            for h, (array, m) in enumerate(sums):
                a = array[0:m, bass.ds(w0, WIN)]
                add = dve.tensor_tensor(a, a, acc_ps[0:m, j % 2, h * WIN:(h + 1) * WIN], ALU.add)
            add.then_inc(sc_add.sem, 1)

        def segments_counted():
            for c in (oh, sc_mm, sc_add):
                c.n += NG
            for c in (oh_x, mm_x, add_x):
                c.n += NG * (N_WIN - 1)

        def clear_acc(halves):
            return [v_done.mark(dve.memset(acc[:, h, :], 0.0)) for h in range(halves)]

        def sum_neighbours(table, ready, with_degree=False):
            wait(dve, *clear_acc(1))
            wait(pool, *ready)
            wait(sp, sc_mm.now(), st_mm.now())
            sums = [(acc[:, 0, :], D)] + ([(deg, 1)] if with_degree else [])
            with nc.Fori(0, NG // UNROLL) as i:
                for j in range(UNROLL):
                    g = i * UNROLL + j
                    load_idx(g, i, j, [src_g], [(sc_mm.sem, sc_mm.n + g - (UNROLL - 1))])
                    gather(i, j, [(table, 0, D)])
                    one_hot(g, j)
                    if j:
                        segment_add(g - 1, j - 1, sums)
                    chans = [(lambda c, j=j: m_ring[:, j, c, 0:D], D)] + (
                        [(lambda c: ones[:, 0:1], 1)] if with_degree else [])
                    segment_mm(g, j, [(rows_in[j].sem, rows_in[j].n + 16 * GC * (i + 1))], chans)
                segment_add(i * UNROLL + UNROLL - 1, UNROLL - 1, sums)
            for j in range(UNROLL):
                idx_in[j].n += 16 * NG // UNROLL
                rows_in[j].n += 16 * GC * NG // UNROLL
            segments_counted()
            return sc_add.now()

        bank_free = [None] * 4
        turn = [0]

        def bank():
            b = turn[0] % 4
            turn[0] += 1
            return b

        def blocks():
            return [(a, min(a + 512, NP)) for a in range(0, NP, 512)]

        def product_T(terms, ready, evacuate):
            wait(pe, *ready)
            marks = []
            for a, b in blocks():
                k = bank()
                if bank_free[k]:
                    wait(pe, bank_free[k])
                for n, (lhs, rhs) in enumerate(terms):
                    mm = pe.matmul(banks[:, k, 0:b - a], lhs, rhs[:, a:b], start=(n == 0), stop=(n == len(terms) - 1))
                done = p_done.mark(mm)
                marks.append((done, k, a, b))
                bank_free[k] = evacuate(banks[:, k, 0:b - a], a, b, done)
                last = bank_free[k]
            return last

        def to_act(out_, func, bias, scale=1.0):
            def evacuate(ps, a, b, done):
                wait(act, done)
                return a_done.mark(act.activation(out_[:, a:b], ps, func, bias=bias, scale=scale))
            return evacuate

        def turn_tiles(src_tile, out_block, ready):
            wait(pe, *ready)
            marks = []
            for t0 in range(0, N_TILES, 4):
                n = min(4, N_TILES - t0)
                k = bank()
                if bank_free[k]:
                    wait(pe, bank_free[k])
                for q in range(n):
                    done = p_done.mark(pe.transpose(banks[:, k, q * D:(q + 1) * D], src_tile(t0 + q), ident[:, :]))
                eng, cnt = (dve, v_done) if (t0 // 4) % 2 else (act, a_done)
                wait(eng, done)
                o, s = out_block(t0, n), banks[:, k, 0:n * D]
                bank_free[k] = cnt.mark(eng.tensor_copy(o, s) if eng is dve else eng.copy(o, s))
                marks.append(bank_free[k])
            return marks[-2:]

        def T_to_N(src, out3, ready):
            return turn_tiles(lambda t: src[:, t * D:(t + 1) * D],
                              lambda t0, n: out3[:, t0:t0 + n, :].rearrange("p t f -> p (t f)"), ready)

        def N_to_T(src3, out_, ready):
            marks = turn_tiles(lambda t: src3[:, t, :], lambda t0, n: out_[:, t0 * D:(t0 + n) * D], ready)
            wait(dve, *marks)
            return [v_done.mark(dve.memset(out_[:, N_NODES:NP], 0.0))]

        def write_table(src3, table, ready):
            wait(sp, *ready)
            return table_w.mark(sp.dma_start(table.rearrange("(t p) f -> p t f", p=D), src3))

        def node_product(src, rhs, width, ready, bias=None):
            wait(pe, *ready)
            per = 512 // width
            marks = []
            for t0 in range(0, N_TILES, per):
                n = min(per, N_TILES - t0)
                k = bank()
                if bank_free[k]:
                    wait(pe, bank_free[k])
                for q in range(n):
                    mm = pe.matmul(banks[:, k, q * width:(q + 1) * width], src[:, (t0 + q) * D:(t0 + q + 1) * D], rhs,
                                   start=True, stop=True)
                done = p_done.mark(mm)
                eng, cnt = (dve, v_done) if (t0 // per) % 2 else (act, a_done)
                wait(eng, done)
                o = tN[:, t0:t0 + n, 0:width]
                s = banks[:, k, 0:n * width].rearrange("p (t f) -> p t f", f=width)
                bank_free[k] = cnt.mark(eng.tensor_copy(o, s) if eng is dve else eng.copy(o, s))
                marks.append(bank_free[k])
            return marks[-2:]

        def norm_N(v3, ready, tmp3):
            mean, var, std, inv = (vec[:, k * N_TILES:(k + 1) * N_TILES] for k in range(4))
            wait(dve, *ready)
            t = v_done.mark(dve.tensor_reduce(mean, v3, AX.X, ALU.add))
            wait(dve, t)
            t = v_done.mark(dve.tensor_scalar(mean, mean, 1.0 / D, None, ALU.mult))
            wait(dve, t)
            t = v_done.mark(dve.tensor_tensor(v3, v3, mean.unsqueeze(2).to_broadcast([D, N_TILES, D]), ALU.subtract))
            wait(act, t)
            t = a_done.mark(act.activation(tmp3, v3, ACT.Square))
            wait(dve, t)
            t = v_done.mark(dve.tensor_reduce(var, tmp3, AX.X, ALU.add))
            wait(act, t)
            t = a_done.mark(act.activation(std, var, ACT.Sqrt, bias=eps_c[:, :], scale=1.0 / D))
            wait(dve, t)
            t = v_done.mark(dve.reciprocal(inv, std))
            wait(dve, t)
            return v_done.mark(dve.tensor_tensor(v3, v3, inv.unsqueeze(2).to_broadcast([D, N_TILES, D]), ALU.mult))

        def add_and_norm(yT, ready):
            y3 = tN[:, :, 0:D]
            marks = T_to_N_wide(yT, ready)
            wait(dve, *marks)
            t = v_done.mark(dve.tensor_tensor(xN[:, :, :], xN[:, :, :], y3, ALU.add))
            return norm_N(xN[:, :, :], [t], y3)

        def T_to_N_wide(src, ready):
            wait(pe, *ready)
            marks = []
            for t0 in range(0, N_TILES, 4):
                n = min(4, N_TILES - t0)
                k = bank()
                if bank_free[k]:
                    wait(pe, bank_free[k])
                for q in range(n):
                    done = p_done.mark(pe.transpose(banks[:, k, q * D:(q + 1) * D],
                                                    src[:, (t0 + q) * D:(t0 + q + 1) * D], ident[:, :]))
                eng, cnt = (dve, v_done) if (t0 // 4) % 2 else (act, a_done)
                wait(eng, done)
                o, s = tN[:, t0:t0 + n, 0:D], banks[:, k, 0:n * D].rearrange("p (t f) -> p t f", f=D)
                bank_free[k] = cnt.mark(eng.tensor_copy(o, s) if eng is dve else eng.copy(o, s))
                marks.append(bank_free[k])
            return marks[-2:]

        one_eps = eps_sb
        wait(dve, in_)
        one = v_done.mark(dve.tensor_scalar(one_eps[:, :], eps_sb[:, :], 1.0, None, ALU.add))

        def gin(layer, inT, wa, ba, g_, bt, wb, bb, func, summed):
            a0 = acc[:, 0, :]
            hid = acc[:, 1, :]
            c = chan
            wait(dve, summed, one)
            t = v_done.mark(dve.scalar_tensor_tensor(out=a0, in0=inT[:, :], scalar=one_eps[:, layer:layer + 1], in1=a0,
                                                     op0=ALU.mult, op1=ALU.add))
            t = product_T([(W(wa), a0)], [t], to_act(hid, ACT.Identity, col(ba)))
            wait(dve, t)
            t = v_done.mark(dve.tensor_reduce(c[:, 0:1], hid[:, 0:N_NODES], AX.X, ALU.add))
            wait(dve, t)
            t = v_done.mark(dve.tensor_scalar(c[:, 1:2], c[:, 0:1], -1.0 / N_NODES, None, ALU.mult))
            wait(act, t)
            t = a_done.mark(act.activation(a0[:, 0:N_NODES], hid[:, 0:N_NODES], ACT.Square, bias=c[:, 1:2],
                                           accum_out=c[:, 2:3]))
            wait(act, t)
            t = a_done.mark(act.activation(c[:, 3:4], c[:, 2:3], ACT.Sqrt, bias=eps_c[:, :], scale=1.0 / N_NODES))
            wait(dve, t)
            t = v_done.mark(dve.reciprocal(c[:, 4:5], c[:, 3:4]))
            wait(dve, t)
            t = v_done.mark(dve.tensor_tensor(c[:, 5:6], c[:, 4:5], col(g_), ALU.mult))
            wait(dve, t)
            t = v_done.mark(dve.scalar_tensor_tensor(out=c[:, 6:7], in0=c[:, 1:2], scalar=c[:, 5:6], in1=col(bt),
                                                     op0=ALU.mult, op1=ALU.add))
            wait(act, t)
            t = a_done.mark(act.activation(a0, hid, ACT.Relu, bias=c[:, 6:7], scale=c[:, 5:6]))
            return product_T([(W(wb), a0)], [t], to_act(tA, func, col(bb)))

        s = sum_neighbours(x_n, [in_], with_degree=True)
        t = gin(0, xT, "w1a", "b1a", "g1", "bt1", "w1b", "b1b", ACT.Relu, s)
        m = T_to_N_wide(tA, [t])
        t1 = write_table(tN[:, :, 0:D], tab0, m)
        s = sum_neighbours(tab0, [t1])
        t = gin(1, tA, "w2a", "b2a", "g2", "bt2", "w2b", "b2b", ACT.Identity, s)
        xn_ready = add_and_norm(tA, [t])
        xt_ready = N_to_T(xN, xT, [xn_ready])

        def block1(xn_ready, xt_ready):
            m = node_product(xT, W("msg_xs"), D, xt_ready)
            t = write_table(tN[:, :, 0:D], tabs, m)
            wait(act, t)
            wait(dve, t)
            m = node_product(xT, W("msg_xd"), D, [])
            wait(dve, *m)
            bias = row("msg_b1").unsqueeze(1).to_broadcast([D, N_TILES, D])
            t = v_done.mark(dve.tensor_tensor(tN[:, :, 0:D], tN[:, :, 0:D], bias, ALU.add))
            t = write_table(tN[:, :, 0:D], tabd, [t])
            wait(dve, *clear_acc(1))
            wait(pool, t)
            wait(sp, sc_mm.now(), st_mm.now())

            def edge_product(i, j):
                g = i * UNROLL + j
                wait(pe, (e_in[j].sem, e_in[j].n + 16 * (i + 1)))
                wait(pe, (pre.sem, pre.n + g - 1))
                for c in range(GC):
                    mm = pe.matmul(banks[:, 2 * (j % 2), c * D:(c + 1) * D], e_ring[:, j, c * D:(c + 1) * D],
                                   W("msg_e"), start=True, stop=True)
                mm.then_inc(ve_mm.sem, 1)

            sums = [(acc[:, 0, :], D)]
            with nc.Fori(0, NG // UNROLL) as i:
                edge_product(i, 0)
                for j in range(UNROLL):
                    g = i * UNROLL + j
                    load_idx(g, i, j, [src_g, dst_g], [(sc_mm.sem, sc_mm.n + g - (UNROLL - 1))])
                    load_e(g, i, j)
                    gather(i, j, [(tabs, 0, D), (tabd, D, D)])
                    wait(dve, (rows_in[j].sem, rows_in[j].n + 32 * GC * (i + 1)))
                    wait(dve, (ve_mm.sem, ve_mm.n + g + 1))
                    a, b = m_ring[:, j, :, 0:D], m_ring[:, j, :, D:2 * D]
                    dve.tensor_tensor(a, a, banks[:, 2 * (j % 2), :].rearrange("p (c f) -> p c f", f=D),
                                      ALU.add).then_inc(msg.sem, 1)
                    one_hot(g, j)
                    wait(dve, (msg.sem, msg.n + g + 1))
                    dve.tensor_tensor(a, a, b, ALU.add).then_inc(pre.sem, 1)
                    if j:
                        segment_add(g - 1, j - 1, sums)
                    wait(act, (pre.sem, pre.n + g + 1))
                    act.activation(a, a, ACT.Silu).then_inc(sq.sem, 1)
                    if j + 1 < UNROLL:
                        edge_product(i, j + 1)
                    segment_mm(g, j, [(sq.sem, sq.n + g + 1)], [(lambda c, j=j: m_ring[:, j, c, 0:D], D)])
                segment_add(i * UNROLL + UNROLL - 1, UNROLL - 1, sums)
            for j in range(UNROLL):
                idx_in[j].n += 32 * NG // UNROLL
                e_in[j].n += 16 * NG // UNROLL
                rows_in[j].n += 32 * GC * NG // UNROLL
            for c in (ve_mm, pre, msg, sq):
                c.n += NG
            segments_counted()
            for k in range(4):
                bank_free[k] = pre.now()

            a0, a1 = acc[:, 0, :], acc[:, 1, :]
            t = product_T([(W("msg_2"), a0), (row("msg_b2")[0:1, :], deg)], [sc_add.now()], to_act(a1, ACT.Identity, 0.0))
            t = product_T([(W("upd_x"), xT), (W("upd_a"), a1)], [t, *xt_ready], to_act(a0, ACT.Silu, col("upd_b1")))
            t = product_T([(W("upd_2"), a0)], [t], to_act(tA, ACT.Identity, col("upd_b2")))
            y3 = tN[:, :, 0:D]
            m = T_to_N_wide(tA, [t])
            wait(dve, *m)
            t = v_done.mark(dve.tensor_tensor(y3, y3, xN[:, :, :], ALU.add))
            t = norm_N(y3, [t], tN[:, :, D:2 * D])
            wait(dve, t)
            t = v_done.mark(dve.tensor_tensor(y3, y3, row("ln_g").unsqueeze(1).to_broadcast([D, N_TILES, D]), ALU.mult))
            wait(dve, t)
            t = v_done.mark(dve.tensor_tensor(y3, y3, row("ln_b").unsqueeze(1).to_broadcast([D, N_TILES, D]), ALU.add))
            wait(dve, t)
            t = v_done.mark(dve.tensor_tensor(xN[:, :, :], xN[:, :, :], y3, ALU.add))
            xn = norm_N(xN[:, :, :], [t], y3)
            return xn, N_to_T(xN, xT, [xn])

        def block2(xn_ready, xt_ready):
            hT, h_ready = xT, list(xt_ready)
            for l in range(N_LAYERS2):
                c = chan
                SG, AB, B1, MEAN, EX2, VAR, S, SH, LOW = (c[:, 2 * k:2 * k + 2] for k in range(9))
                gam, bet, b1 = (col_all[:, COLS.index(f"{k}{l}0"):COLS.index(f"{k}{l}0") + 2] for k in ("g", "bt", "b"))
                t = v_done.mark(dve.tensor_scalar(SG, gam, 0.0, 2.0, ALU.is_ge, ALU.mult))
                wait(dve, t)
                t = v_done.mark(dve.tensor_scalar(SG, SG, -1.0, None, ALU.add))
                wait(dve, t)
                v_done.mark(dve.tensor_tensor(B1, SG, b1, ALU.mult))
                t = v_done.mark(dve.tensor_tensor(AB, SG, gam, ALU.mult))
                wait(dve, t)
                t = v_done.mark(dve.tensor_scalar(AB, AB, TINY, None, ALU.max))

                def spread(cols2, dst, t):
                    for h in range(2):
                        wait(dve, t)
                        t = v_done.mark(dve.tensor_scalar(diag[:, :], ident[:, :], cols2[:, h:h + 1], None, ALU.mult))
                        wait(pe, t)
                        t = p_done.mark(pe.matmul(x_ps[:, 0:D], ones[:, :], diag[:, :], start=True, stop=True))
                        wait(dve, t)
                        t = v_done.mark(dve.tensor_copy(dst[:, h * D:(h + 1) * D], x_ps[:, 0:D]))
                    return t

                t = spread(SG, sgn, t)
                wait(dve, t)
                v_done.mark(dve.tensor_tensor(W(f"eh{l}"), W(f"eh{l}"), sgn[:, :], ALU.mult))
                t = v_done.mark(dve.tensor_tensor(W(f"ee{l}"), W(f"ee{l}"), sgn[:, :], ALU.mult))
                m = node_product(hT, W(f"eh{l}"), 2 * D, [t] + h_ready)
                t = write_table(tN[:, :, :], tab2, m)
                wait(pool, t)
                wait(sp, sc_mm.now(), st_mm.now())
                t = v_done.mark(dve.memset(small[:, 8:12], 0.0))
                wait(pe, t)
                pe.matmul(st_ps[:, 0:4], ones[:, :], small[:, 8:12], start=True, stop=False, skip_group_check=True)

                def relu_e(i, j):
                    if l:
                        g = i * UNROLL + j
                        hold(act, (e_in[j].sem, e_in[j].n + 16 * (i + 1)))
                        act.activation(e_ring[:, j, :], e_ring[:, j, :], ACT.Relu).then_inc(e_relu.sem, 1)

                def edge_product(i, j):
                    g = i * UNROLL + j
                    if l:
                        wait(pe, (e_relu.sem, e_relu.n + g + 1))
                    else:
                        wait(pe, (e_in[j].sem, e_in[j].n + 16 * (i + 1)))
                    wait(pe, (pre.sem, pre.n + g - 1))
                    for c_ in range(GC):
                        mm = pe.matmul(banks[:, 2 * (j % 2) + c_ // 2, (c_ % 2) * 256:(c_ % 2) * 256 + 256],
                                       e_ring[:, j, c_ * D:(c_ + 1) * D], W(f"ee{l}"), start=True, stop=True)
                    mm.then_inc(ve_mm.sem, 1)

                with nc.Fori(0, NG // UNROLL) as i:
                    relu_e(i, 0)
                    edge_product(i, 0)
                    for j in range(UNROLL):
                        g = i * UNROLL + j
                        load_idx(g, i, j, [src_g], [(st_mm.sem, st_mm.n + g - (UNROLL - 1)),
                                                    (pre_out[j].sem, pre_out[j].n + 16 * i)])
                        load_e(g, i, j)
                        gather(i, j, [(tab2, 0, 2 * D)])
                        wait(dve, (rows_in[j].sem, rows_in[j].n + 16 * GC * (i + 1)))
                        wait(dve, (ve_mm.sem, ve_mm.n + g + 1))
                        p = m_ring[:, j, :, :].rearrange("p c f -> p (c f)")
                        v = banks[:, 2 * (j % 2):2 * (j % 2) + 2, :].rearrange("p b f -> p (b f)")
                        dve.tensor_tensor(p, p, v, ALU.add).then_inc(pre.sem, 1)
                        if j + 1 < UNROLL:
                            relu_e(i, j + 1)
                            edge_product(i, j + 1)
                        hold(act, (pre.sem, pre.n + g + 1))
                        act.dma_start(pre_dram[bass.ds(g, 1), :, :].rearrange("a p k -> (a p) k"), p
                                      ).then_inc(pre_out[j].sem, 16)
                        wait(act, (st_mm.sem, st_mm.n + g - 1))
                        act.activation(sq_ring[:, j % 2, :, :].rearrange("p c f -> p (c f)"), p, ACT.Square
                                       ).then_inc(sq.sem, 1)
                        wait(pe, (sq.sem, sq.n + g + 1))
                        for c_ in range(GC):
                            for k, a in enumerate((m_ring[:, j, c_, 0:D], m_ring[:, j, c_, D:2 * D],
                                                   sq_ring[:, j % 2, c_, 0:D], sq_ring[:, j % 2, c_, D:2 * D])):
                                mm = pe.matmul(st_ps[:, k:k + 1], a, ones[:, 0:1], start=False, stop=False,
                                               skip_group_check=True)
                        mm.then_inc(st_mm.sem, 1)
                for j in range(UNROLL):
                    idx_in[j].n += 16 * NG // UNROLL
                    e_in[j].n += 16 * NG // UNROLL
                    rows_in[j].n += 16 * GC * NG // UNROLL
                    pre_out[j].n += 16 * NG // UNROLL
                for q in (ve_mm, pre, sq, st_mm) + ((e_relu,) if l else ()):
                    q.n += NG
                for k in range(4):
                    bank_free[k] = pre.now()

                wait(dve, st_mm.now())
                v_done.mark(dve.tensor_scalar(MEAN, st_ps[:, 0:2], 1.0 / N_EDGES, None, ALU.mult))
                t = v_done.mark(dve.tensor_scalar(EX2, st_ps[:, 2:4], 1.0 / N_EDGES, None, ALU.mult))
                wait(dve, t)
                t = v_done.mark(dve.tensor_tensor(VAR, MEAN, MEAN, ALU.mult))
                wait(dve, t)
                t = v_done.mark(dve.tensor_tensor(VAR, EX2, VAR, ALU.subtract))
                wait(dve, t)
                t = v_done.mark(dve.tensor_scalar(VAR, VAR, 0.0, None, ALU.max))
                wait(act, t)
                t = a_done.mark(act.activation(S, VAR, ACT.Sqrt, bias=eps_c[:, :]))
                wait(dve, t)
                t = v_done.mark(dve.reciprocal(S, S))
                t = v_done.mark(dve.tensor_tensor(MEAN, MEAN, B1, ALU.add))
                wait(dve, t)
                t = v_done.mark(dve.tensor_tensor(SH, B1, MEAN, ALU.subtract))
                wait(dve, t)
                t = v_done.mark(dve.tensor_tensor(S, S, AB, ALU.mult))
                wait(dve, t)
                t = v_done.mark(dve.reciprocal(LOW, S))
                wait(dve, t)
                t = v_done.mark(dve.tensor_tensor(LOW, LOW, bet, ALU.mult))
                wait(dve, t)
                t = v_done.mark(dve.tensor_tensor(LOW, LOW, SH, ALU.add))
                wait(dve, t)
                t = v_done.mark(dve.tensor_scalar(LOW, LOW, -1.0, None, ALU.mult))
                v_done.mark(dve.tensor_tensor(SH, SH, S, ALU.mult))
                wait(dve, v_done.now())
                v_done.mark(dve.tensor_tensor(SH, SH, bet, ALU.add))
                t = spread(LOW, low, v_done.now())

                wait(dve, t, *clear_acc(2))
                wait(sp, *[q.now() for q in pre_out], st_mm.now(), sc_mm.now())
                sums = [(acc[:, 0, :], D), (acc[:, 1, :], D)]
                with nc.Fori(0, NG // UNROLL) as i:
                    for j in range(UNROLL):
                        g = i * UNROLL + j
                        p = m_ring[:, j, :, :]
                        hold(sp, (sc_mm.sem, sc_mm.n + g - (UNROLL - 1)))
                        sp.dma_start(p.rearrange("p c f -> p (c f)"),
                                     pre_dram[bass.ds(g, 1), :, :].rearrange("a p k -> (a p) k")
                                     ).then_inc(pre_in[j].sem, 16)
                        one_hot(g, j)
                        wait(dve, (pre_in[j].sem, pre_in[j].n + 16 * (i + 1)))
                        dve.tensor_tensor(p, p, low[:, :].unsqueeze(1).to_broadcast([D, GC, 2 * D]), ALU.max
                                          ).then_inc(msg.sem, 1)
                        if j:
                            segment_add(g - 1, j - 1, sums)
                        segment_mm(g, j, [(msg.sem, msg.n + g + 1)],
                                   [(lambda c_, j=j: m_ring[:, j, c_, 0:D], D),
                                    (lambda c_, j=j: m_ring[:, j, c_, D:2 * D], D)])
                    segment_add(i * UNROLL + UNROLL - 1, UNROLL - 1, sums)
                for j in range(UNROLL):
                    pre_in[j].n += 16 * NG // UNROLL
                msg.n += NG
                segments_counted()

                wait(pe, v_done.now())
                pe.matmul(x_ps[0:1, 0:D], SH[:, 0:1], W(f"eo_lo{l}"), start=True, stop=False)
                t = p_done.mark(pe.matmul(x_ps[0:1, 0:D], SH[:, 1:2], W(f"eo_hi{l}"), start=False, stop=True))
                wait(dve, t)
                v_done.mark(dve.tensor_tensor(v_row[:, :], x_ps[0:1, 0:D], row(f"eo_b{l}")[0:1, :], ALU.add))
                v_done.mark(dve.tensor_scalar(W(f"eo_lo{l}"), W(f"eo_lo{l}"), S[:, 0:1], None, ALU.mult))
                t = v_done.mark(dve.tensor_scalar(W(f"eo_hi{l}"), W(f"eo_hi{l}"), S[:, 1:2], None, ALU.mult))
                func = ACT.Relu if l < N_LAYERS2 - 1 else ACT.Identity
                t = product_T([(W(f"eo_lo{l}"), acc[:, 0, :]), (W(f"eo_hi{l}"), acc[:, 1, :]), (v_row[:, :], deg)],
                              [t, sc_add.now()], to_act(tA, func, 0.0))
                hT, h_ready = tA, [t]
                wait(dve, t)
            xn = add_and_norm(tA, h_ready)
            return xn, None

        def block3(xn_ready):
            t = write_table(xN[:, :, :], tab0, [xn_ready])
            for layer, (w, b) in enumerate((("sage1", "sage_b1"), ("sage2", "sage_b2"))):
                s = sum_neighbours(tab0, [t])
                t = product_T([(W(w), acc[:, 0, :])], [s], to_act(tA, ACT.Relu, col(b)))
                if layer == 0:
                    m = T_to_N_wide(tA, [t])
                    t = write_table(tN[:, :, 0:D], tab0, m)
            return add_and_norm(tA, [t])

        stages = [lambda: None]
        if stop_at is None or stop_at > 1:
            xn_ready, xt_ready = block1(xn_ready, xt_ready)
        if stop_at is None or stop_at > 2:
            xn_ready, _ = block2(xn_ready, xt_ready)
        if stop_at is None or stop_at > 3:
            xn_ready = block3(xn_ready)

        wait(sp, xn_ready)
        full = N_NODES // D
        out_w.mark(sp.dma_start(out[0:full * D, :].rearrange("(t p) f -> p t f", p=D), xN[:, 0:full, :]))
        out_w.mark(sp.dma_start(out[full * D:N_NODES, :], xN[0:N_NODES - full * D, full, :]))
        wait(sp, out_w.now(), table_w.now(), *[q.now() for q in pre_out])


WIDE_FROM = WIN


def kernel(**inputs):
    import numpy as np
    import concourse.bacc as bacc
    from concourse.bass_utils import run_bass_kernel_spmd

    a = {k: np.asarray(v) for k, v in inputs.items()}

    def padded(v, shape, fill):
        o = np.full(shape, fill, v.dtype)
        o[tuple(slice(0, n) for n in v.shape)] = v
        return o

    x = padded(a["x"], (NP, D), 0)
    src = padded(a["src"], (EP,), NP - 1).reshape(NG, GC, D)
    dst = padded(a["dst"], (EP,), -1).reshape(NG, GC, D)
    dst_ok = padded(a["dst"], (EP,), NP - 1).reshape(NG, GC, D)
    w = {"w1a": a["L0_gnn_w1a"], "w1b": a["L0_gnn_w1b"], "w2a": a["L0_gnn_w2a"], "w2b": a["L0_gnn_w2b"],
         "msg_xs": a["L1_gnn_msg_W1"][0:D], "msg_xd": a["L1_gnn_msg_W1"][D:2 * D], "msg_e": a["L1_gnn_msg_W1"][2 * D:],
         "msg_2": a["L1_gnn_msg_W2"], "upd_x": a["L1_gnn_upd_W1"][0:D], "upd_a": a["L1_gnn_upd_W1"][D:],
         "upd_2": a["L1_gnn_upd_W2"], "sage1": a["L3_gnn_W1"].T, "sage2": a["L3_gnn_W2"].T}
    c = {"b1a": a["L0_gnn_b1a"], "g1": a["L0_gnn_g1"], "bt1": a["L0_gnn_bt1"], "b1b": a["L0_gnn_b1b"],
         "b2a": a["L0_gnn_b2a"], "g2": a["L0_gnn_g2"], "bt2": a["L0_gnn_bt2"], "b2b": a["L0_gnn_b2b"],
         "upd_b1": a["L1_gnn_upd_b1"], "upd_b2": a["L1_gnn_upd_b2"], "sage_b1": a["L3_gnn_b1"], "sage_b2": a["L3_gnn_b2"]}
    r = {"msg_b1": a["L1_gnn_msg_b1"], "msg_b2": a["L1_gnn_msg_b2"], "ln_g": a["L1_gnn_ln_gamma"],
         "ln_b": a["L1_gnn_ln_beta"]}
    for l in range(N_LAYERS2):
        w1, w2 = a["L2_gnn_W1"][l].T, a["L2_gnn_W2"][l].T
        w |= {f"eh{l}": w1[0:D], f"ee{l}": w1[D:], f"eo_lo{l}": w2[0:D], f"eo_hi{l}": w2[D:]}
        for h in range(2):
            part = slice(h * D, (h + 1) * D)
            c |= {f"b{l}{h}": a["L2_gnn_b1"][l][part], f"g{l}{h}": a["L2_gnn_gamma"][l][part],
                  f"bt{l}{h}": a["L2_gnn_beta"][l][part]}
        r[f"eo_b{l}"] = a["L2_gnn_b2"][l]
    arrays = {
        "x_n": x, "x_t": x.T, "e_t": padded(a["edge_attr_128"], (EP, D), 0).T,
        "src_g": src.transpose(0, 2, 1), "dst_g": dst_ok.transpose(0, 2, 1),
        "dst_p": dst.reshape(NG * GC, D).T,
        "weights": np.concatenate([w[k] for k in WEIGHTS], axis=1),
        "cols": np.stack([c[k] for k in COLS], axis=1), "rows": np.stack([r[k] for k in ROWS]),
        "eps": np.stack([a["L0_gnn_eps1"], a["L0_gnn_eps2"]]).reshape(1, 2),
    }
    arrays = {k: np.ascontiguousarray(v) for k, v in arrays.items()}
    nc = bacc.Bacc("TRN2", target_bir_lowering=False, num_devices=1)
    args = [nc.dram_tensor(k, v.shape, mybir.dt.from_np(v.dtype), kind="ExternalInput").ap() for k, v in arrays.items()]
    o = nc.dram_tensor("out", (N_NODES, D), F32, kind="ExternalOutput").ap()
    build(nc, *args, o)
    return run_bass_kernel_spmd(nc, [arrays], core_ids=[0]).results[0]["out"]
```

```python
from contextlib import ExitStack

import concourse.bass as bass
from concourse import mybir

F32 = mybir.dt.float32
I32 = mybir.dt.int32
ALU = mybir.AluOpType
ACT = mybir.ActivationFunctionType
AX = mybir.AxisListType

D = 128
N_NODES = 3125
N_TILES = -(-N_NODES // D)
NP = N_TILES * D
N_EDGES = 53125
GC = 4
GE = GC * D
NG = -(-N_EDGES // GE)
EP = NG * GE
WIN = 64
N_WIN = NP // WIN
UNROLL = 8
E_SLOTS = 4
W0_AHEAD = 4
EPS = 1e-5
TINY = 1e-30
N_LAYERS2 = 3

WEIGHTS, _at = {}, 0
for _n, _w in ([("w1a", 1), ("w1b", 1), ("w2a", 1), ("w2b", 1), ("msg_xs", 1), ("msg_xd", 1), ("msg_e", 1),
                ("msg_2", 1), ("upd_x", 1), ("upd_a", 1), ("upd_2", 1), ("sage1", 1), ("sage2", 1)]
               + [(f"{k}{l}", w) for l in range(N_LAYERS2) for k, w in
                  (("eh", 2), ("ee", 2), ("eo_lo", 1), ("eo_hi", 1))]):
    WEIGHTS[_n] = (_at, _w * D)
    _at += _w * D
W_COLS = _at
COLS = ["b1a", "g1", "bt1", "b1b", "b2a", "g2", "bt2", "b2b", "upd_b1", "upd_b2", "sage_b1", "sage_b2"] + [
    f"{k}{l}{h}" for l in range(N_LAYERS2) for k in ("b", "g", "bt") for h in (0, 1)]
ROWS = ["msg_b1", "msg_b2", "ln_g", "ln_b"] + [f"eo_b{l}" for l in range(N_LAYERS2)]


class Count:

    def __init__(self, sem, by=1):
        self.sem, self.by, self.n = sem, by, 0

    def mark(self, ins):
        ins.then_inc(self.sem, self.by)
        self.n += self.by
        return (self.sem, self.n)

    def now(self):
        return (self.sem, self.n)


def wait(eng, *marks):
    for sem, value in marks:
        eng.wait_ge(sem, value)


def hold(eng, *marks):
    for mark in marks:
        wait(eng, mark)
        eng.nop(nofuse=True)


def build(nc, x_n, x_t, e_t, src_g, dst_g, dst_p, weights, cols, rows, eps, out, stop_at=None):
    pe, dve, act, pool, sp = nc.tensor, nc.vector, nc.scalar, nc.gpsimd, nc.sync
    with ExitStack() as ctx:
        def sb(name, shape, dt=F32):
            return ctx.enter_context(nc.sbuf_tensor(name, shape, dt))

        def sem(name):
            return ctx.enter_context(nc.semaphore(name))

        def dram(name, shape):
            return nc.dram_tensor(name, shape, F32, kind="Internal").ap()

        w_all = sb("w_all", [D, W_COLS])
        col_all = sb("col_all", [D, len(COLS)])
        row_all = sb("row_all", [D, len(ROWS) * D])
        eps_sb = sb("eps_sb", [D, 2])
        ident = sb("ident", [D, D])
        ones = sb("ones", [D, D])
        eps_c = sb("eps_c", [D, 1])
        node_no = sb("node_no", [D, NP])
        node_no_i = sb("node_no_i", [D, WIN], I32)
        dst_i = sb("dst_i", [D, NG * GC], I32)
        dst_rel = sb("dst_rel", [D, NG * GC])
        w0_i = sb("w0_i", [1, NG], I32)
        any_wide = sb("any_wide", [1, 1], I32)
        small = sb("small", [D, 64])
        diag = sb("diag", [D, D])
        xT = sb("xT", [D, NP])
        xN = sb("xN", [D, N_TILES, D])
        acc = sb("acc", [D, 2, NP])
        deg = sb("deg", [1, NP])
        tA = sb("tA", [D, NP])
        tN = sb("tN", [D, N_TILES, 2 * D])
        vec = sb("vec", [D, 4 * N_TILES])
        m_half = sb("m_half", [D, UNROLL // 2, GC, 2 * D])
        e_ring = sb("e_ring", [D, E_SLOTS, GE])
        idx_ring = sb("idx_ring", [D, UNROLL, 2, GC], I32)
        oh_ring = sb("oh_ring", [D, 2, GC, WIN])
        oh_wide = sb("oh_wide", [D, GC, WIN])
        sq_ring = sb("sq_ring", [D, 2, GC * 2 * D])
        win_ring = sb("win_ring", [WIN, 2, 2 * D])
        sums_row = sb("sums_row", [1, 512])
        sgn = sb("sgn", [D, 2 * D])
        low = sb("low", [D, 2 * D])
        v_row = sb("v_row", [1, D])
        chan = sb("chan", [D, 32])

        banks = ctx.enter_context(nc.psum_tensor("banks", [D, 4, 512], F32))
        acc_ps = ctx.enter_context(nc.psum_tensor("acc_ps", [D, 2, 512], F32))
        st_ps = ctx.enter_context(nc.psum_tensor("st_ps", [D, 512], F32))
        x_ps = ctx.enter_context(nc.psum_tensor("x_ps", [D, 512], F32))

        tab0 = dram("tab0", [NP, D])
        tabs = dram("tabs", [NP, D])
        tabd = dram("tabd", [NP, D])
        tab2 = dram("tab2", [NP, 2 * D])
        pre_dram = dram("pre_dram", [NG, D, GC * 2 * D])

        m_ring = [m_half[:, j, :, :] for j in range(UNROLL // 2)] + [
            tN[:, j * GC:(j + 1) * GC, :] for j in range(UNROLL // 2)]

        v_done, a_done, p_done, g_done = (Count(sem(s)) for s in ("v_done", "a_done", "p_done", "g_done"))
        loaded = Count(sem("loaded"), 16)
        table_w = Count(sem("table_w"), 16)
        out_w = Count(sem("out_w"), 16)
        idx_in = [Count(sem(f"idx_in{j}"), 16) for j in range(UNROLL)]
        e_in = [Count(sem(f"e_in{j}"), 16) for j in range(E_SLOTS)]
        rows_in = [Count(sem(f"rows_in{j}"), 16) for j in range(UNROLL)]
        pre_in = [Count(sem(f"pre_in{j}"), 16) for j in range(UNROLL)]
        pre_out = [Count(sem(f"pre_out{j}"), 16) for j in range(UNROLL)]
        e_relu = Count(sem("e_relu"))
        ve_mm = Count(sem("ve_mm"))
        pre = Count(sem("pre"))
        msg = Count(sem("msg"))
        sq = Count(sem("sq"))
        st_mm = Count(sem("st_mm"))
        sq_add = Count(sem("sq_add"))
        win_out = Count(sem("win_out"))
        win_t = Count(sem("win_t"))
        oh = Count(sem("oh"))
        sc_mm = Count(sem("sc_mm"))
        sc_add = Count(sem("sc_add"))
        oh_x, mm_x, add_x = (Count(sem(s)) for s in ("oh_x", "mm_x", "add_x"))

        def W(name, a=0, b=None):
            at, width = WEIGHTS[name]
            return w_all[:, at + a:at + (width if b is None else b)]

        def col(name):
            i = COLS.index(name)
            return col_all[:, i:i + 1]

        def row(name):
            i = ROWS.index(name)
            return row_all[:, i * D:(i + 1) * D]

        for q, (c, k) in enumerate(((sc_mm, UNROLL), (st_mm, UNROLL), (sq, UNROLL), (ve_mm, E_SLOTS), (pre, 2), (sc_add, 2),
                                 (sq_add, 2), (win_out, 2), (win_t, 2))):
            pool.memset(small[:, 16 + q:17 + q], 0.0).then_inc(c.sem, k)
            c.n = k
        g_done.mark(pool.memset(small[:, 0:1], 0.0))

        for dst, src in ((dst_i[:, :], dst_p), (xN[:, :, :], x_n.rearrange("(t p) f -> p t f", p=D)),
                         (row_all[:, :], rows.partition_broadcast(D).rearrange("p a f -> p (a f)")),
                         (eps_sb[:, :], eps.partition_broadcast(D).rearrange("p a f -> p (a f)"))):
            loaded.mark(sp.dma_start(dst, src))
        parts = [(xT[:, :], x_t), (col_all[:, :], cols)] + [
            (w_all[:, k * W_COLS // 6:(k + 1) * W_COLS // 6], weights[:, k * W_COLS // 6:(k + 1) * W_COLS // 6])
            for k in range(6)]
        for q, (dst, src) in zip(pre_out, parts):
            q.mark(act.dma_start(dst, src))
        in_ = (loaded.now(), *[q.now() for q in pre_out])
        wait(pool, g_done.now())
        g_done.mark(pool.iota(node_no_i[:, :], [[1, WIN]], base=0, channel_multiplier=0))
        g_done.mark(pool.memset(ones[:, :], 1.0))
        g_done.mark(pool.memset(eps_c[:, :], EPS))
        z = g_done.mark(pool.memset(ident[:, :], 0.0))
        wait(pool, z)
        consts = g_done.mark(pool.affine_select(out=ident[:, :], in_=ident[:, :], compare_op=ALU.not_equal, fill=1.0,
                                                base=0, pattern=[[-1, D]], channel_multiplier=1))
        wait(dve, consts)
        t = v_done.mark(dve.tensor_copy(node_no[:, 0:WIN], node_no_i[:, :]))
        for k in range(1, N_WIN):
            wait(dve, t)
            last = v_done.mark(dve.tensor_scalar(node_no[:, k * WIN:(k + 1) * WIN], node_no[:, 0:WIN],
                                                 float(k * WIN), None, ALU.add))
        deg0 = v_done.mark(dve.memset(deg[:, :], 0.0))

        wait(dve, *in_)
        t = v_done.mark(dve.tensor_copy(dst_rel[:, :], dst_i[:, :]))
        wait(dve, t)
        big = tA[:, 0:NG * GC]
        t = v_done.mark(dve.tensor_scalar(big, dst_rel[:, :], 0.0, 2.0 * NP, ALU.is_lt, ALU.mult))
        wait(dve, t)
        t = v_done.mark(dve.tensor_tensor(big, big, dst_rel[:, :], ALU.add))
        wait(dve, t)
        gmm = tA[:, 512:512 + 2 * NG]
        v_done.mark(dve.tensor_reduce(gmm[:, 0:NG], big.rearrange("p (g k) -> p g k", k=GC), AX.X, ALU.min))
        t = v_done.mark(dve.tensor_reduce(gmm[:, NG:2 * NG], dst_rel[:, :].rearrange("p (g k) -> p g k", k=GC),
                                          AX.X, ALU.max))
        wait(pe, t, consts)
        for h in range(2):
            t = p_done.mark(pe.transpose(x_ps[0:NG, h * D:(h + 1) * D], gmm[:, h * NG:(h + 1) * NG], ident[:, :]))
        wait(dve, t)
        v_done.mark(dve.tensor_reduce(small[0:NG, 1:2], x_ps[0:NG, 0:D], AX.X, ALU.min))
        t = v_done.mark(dve.tensor_reduce(small[0:NG, 2:3], x_ps[0:NG, D:2 * D], AX.X, ALU.max))
        wait(dve, t)
        t = v_done.mark(dve.tensor_tensor(small[0:NG, 3:4], small[0:NG, 2:3], small[0:NG, 1:2], ALU.subtract))
        wait(dve, t)
        t = v_done.mark(dve.tensor_scalar(small[0:NG, 4:5], small[0:NG, 3:4], float(WIDE_FROM), None, ALU.is_ge))
        wait(pe, t)
        t = p_done.mark(pe.matmul(x_ps[:, 256:257], ones[0:NG, :], small[0:NG, 4:5], start=True, stop=True))
        wait(dve, t)
        v_done.mark(dve.tensor_copy(any_wide[:, :], x_ps[0:1, 256:257]))
        t = v_done.mark(dve.tensor_scalar(small[0:NG, 5:6], x_ps[0:NG, 256:257], 0.0, None, ALU.is_equal))
        wait(dve, t)
        t = v_done.mark(dve.tensor_tensor(small[0:NG, 6:7], small[0:NG, 5:6], small[0:NG, 1:2], ALU.mult))
        wait(dve, t)
        t = v_done.mark(dve.tensor_scalar(diag[0:NG, 0:NG], ident[0:NG, 0:NG], small[0:NG, 6:7], None, ALU.mult))
        wait(pe, t)
        t = p_done.mark(pe.matmul(x_ps[:, 0:NG], ones[0:NG, :], diag[0:NG, 0:NG], start=True, stop=True))
        wait(dve, t)
        v_done.mark(dve.tensor_copy(w0_i[:, :], x_ps[0:1, 0:NG]))
        d3 = dst_rel[:, :].rearrange("p (g k) -> p g k", k=GC)
        windows = v_done.mark(dve.tensor_tensor(d3, d3, x_ps[:, 0:NG].unsqueeze(2).to_broadcast([D, NG, GC]),
                                                ALU.subtract))
        wait(dve, windows)
        wait(pe, windows)
        wide_v = dve.value_load(any_wide[0:1, 0:1], min_val=0, max_val=NG)
        wide_p = pe.value_load(any_wide[0:1, 0:1], min_val=0, max_val=NG)

        def load_idx(g, j, srcs, done):
            hold(sp, (done.sem, done.n + g - (UNROLL - 1)))
            for k, a in enumerate(srcs):
                sp.dma_start(idx_ring[:, j, k, :], a[bass.ds(g, 1), :, :].rearrange("a p k -> (a p) k")
                             ).then_inc(idx_in[j].sem, 16)

        def gather(i, j, tables, free):
            hold(pool, (idx_in[j].sem, idx_in[j].n + 16 * len(tables) * (i + 1)), *free)
            for k, (table, at, width) in enumerate(tables):
                for c in range(GC):
                    pool.indirect_dma_start(m_ring[j][:, c, at:at + width], None, table[:, :],
                                            bass.IndirectOffsetOnAxis(ap=idx_ring[:, j, k, c:c + 1], axis=0)
                                            ).then_inc(rows_in[j].sem, 16)

        def rows_ready(i, j, tables=1):
            return (rows_in[j].sem, rows_in[j].n + 16 * GC * tables * (i + 1))

        def e_ready(i, j):
            q = e_in[j % E_SLOTS]
            return (q.sem, q.n + 16 * (i * (UNROLL // E_SLOTS) + j // E_SLOTS + 1))

        def load_e(g, j):
            hold(sp, (ve_mm.sem, ve_mm.n + g - (E_SLOTS - 1)))
            sp.dma_start(e_ring[:, j % E_SLOTS, :], e_t[:, bass.ds(g * GE, GE)]).then_inc(e_in[j % E_SLOTS].sem, 16)

        def window_starts(i, j0, w0):
            w0 |= {j: dve.value_load(w0_i[0:1, bass.ds(i * UNROLL + j, 1)], min_val=0, max_val=N_NODES - 1)
                   for j in range(j0, j0 + W0_AHEAD)}

        def one_hot(g, j):
            wait(dve, (sc_mm.sem, sc_mm.n + g - 1))
            dve.tensor_tensor(oh_ring[:, j % 2, :, :], node_no[:, 0:WIN].unsqueeze(1).to_broadcast([D, GC, WIN]),
                              dst_rel[:, bass.ds(g * GC, GC)].unsqueeze(2).to_broadcast([D, GC, WIN]),
                              ALU.is_equal).then_inc(oh.sem, 1)

        def wide_mm(g, channels):
            with pe.If(wide_p > 0):
                with pe.Fori(1, N_WIN) as k:
                    at = g * (N_WIN - 1) + k
                    wait(pe, (oh_x.sem, oh_x.n + at))
                    for h, (lhs, m) in enumerate(channels):
                        for c in range(GC):
                            mm = pe.matmul(x_ps[0:m, h * WIN:(h + 1) * WIN], lhs(c), oh_wide[:, c, :],
                                           start=(c == 0), stop=(c == GC - 1))
                    mm.then_inc(mm_x.sem, 1)

        def wide_add(g, sums):
            with dve.If(wide_v > 0):
                with dve.Fori(1, N_WIN) as k:
                    at = g * (N_WIN - 1) + k
                    dve.tensor_tensor(oh_wide[:, :, :],
                                      node_no[:, bass.ds(k * WIN, WIN)].unsqueeze(1).to_broadcast([D, GC, WIN]),
                                      dst_rel[:, bass.ds(g * GC, GC)].unsqueeze(2).to_broadcast([D, GC, WIN]),
                                      ALU.is_equal).then_inc(oh_x.sem, 1)
                    wait(dve, (mm_x.sem, mm_x.n + at))
                    for h, (array, m) in enumerate(sums):
                        a = array[0:m, bass.ds(k * WIN, WIN)]
                        add = dve.tensor_tensor(a, a, x_ps[0:m, h * WIN:(h + 1) * WIN], ALU.add)
                    add.then_inc(add_x.sem, 1)
                    wait(dve, (add_x.sem, add_x.n + at))

        def segment_mm(g, j, ready, channels):
            wait(pe, *ready)
            wide_mm(g, channels)
            wait(pe, (oh.sem, oh.n + g + 1))
            wait(pe, (sc_add.sem, sc_add.n + g - 1))
            for h, (lhs, m) in enumerate(channels):
                for c in range(GC):
                    mm = pe.matmul(acc_ps[0:m, j % 2, h * WIN:(h + 1) * WIN], lhs(c), oh_ring[:, j % 2, c, :],
                                   start=(c == 0), stop=(c == GC - 1))
            mm.then_inc(sc_mm.sem, 1)

        def segment_add(g, w0, product, ps, sums):
            wait(dve, (product.sem, product.n + g + 1))
            wait(dve, (sc_add.sem, sc_add.n + g))
            for h, (array, m) in enumerate(sums):
                a = array[0:m, bass.ds(w0, WIN)]
                add = dve.tensor_tensor(a, a, ps[0:m, h * WIN:(h + 1) * WIN], ALU.add)
            add.then_inc(sc_add.sem, 1)

        def segments_counted():
            for c in (oh, sc_mm, sc_add):
                c.n += NG
            for c in (oh_x, mm_x, add_x):
                c.n += NG * (N_WIN - 1)

        def rings_counted(idx=0, e=0, rows=0, pre_o=0, pre_i=0):
            for qs, k in ((idx_in, idx), (e_in, e), (rows_in, GC * rows), (pre_out, pre_o), (pre_in, pre_i)):
                for q in qs:
                    q.n += 16 * k * NG // len(qs)

        def clear_acc(halves):
            return [v_done.mark(dve.memset(acc[:, h, :], 0.0)) for h in range(halves)]

        def sum_neighbours(table, ready, with_degree=False):
            wait(dve, *clear_acc(1))
            wait(pool, *ready)
            wait(sp, sc_mm.now(), st_mm.now())
            sums = [(acc[:, 0, :], D)] + ([(deg, 1)] if with_degree else [])
            with nc.Fori(0, NG // UNROLL) as i:
                w0 = {}
                for j in range(UNROLL):
                    g = i * UNROLL + j
                    if j % W0_AHEAD == 0:
                        window_starts(i, j, w0)
                    load_idx(g, j, [src_g], sc_mm)
                    gather(i, j, [(table, 0, D)], [(sc_mm.sem, sc_mm.n + g - (UNROLL - 1))])
                    wide_add(g, sums)
                    one_hot(g, j)
                    if j:
                        segment_add(g - 1, w0[j - 1], sc_mm, acc_ps[:, (j - 1) % 2, :], sums)
                    chans = [(lambda c, j=j: m_ring[j][:, c, 0:D], D)] + (
                        [(lambda c: ones[:, 0:1], 1)] if with_degree else [])
                    segment_mm(g, j, [rows_ready(i, j)], chans)
                segment_add(g, w0[j], sc_mm, acc_ps[:, j % 2, :], sums)
            rings_counted(idx=1, rows=1)
            segments_counted()
            return sc_add.now()

        bank_free = [None] * 4
        turn = [0]

        def bank():
            b = turn[0] % 4
            turn[0] += 1
            return b

        def blocks():
            return [(a, min(a + 512, NP)) for a in range(0, NP, 512)]

        def product_T(terms, ready, evacuate):
            wait(pe, *ready)
            marks = []
            for a, b in blocks():
                k = bank()
                if bank_free[k]:
                    wait(pe, bank_free[k])
                for n, (lhs, rhs) in enumerate(terms):
                    mm = pe.matmul(banks[:, k, 0:b - a], lhs, rhs[:, a:b], start=(n == 0), stop=(n == len(terms) - 1))
                done = p_done.mark(mm)
                marks.append((done, k, a, b))
                bank_free[k] = evacuate(banks[:, k, 0:b - a], a, b, done)
                last = bank_free[k]
            return last

        def to_act(out_, func, bias, scale=1.0):
            def evacuate(ps, a, b, done):
                wait(act, done)
                return a_done.mark(act.activation(out_[:, a:b], ps, func, bias=bias, scale=scale))
            return evacuate

        def turn_tiles(src_tile, out_block, ready):
            wait(pe, *ready)
            marks = []
            for t0 in range(0, N_TILES, 4):
                n = min(4, N_TILES - t0)
                k = bank()
                if bank_free[k]:
                    wait(pe, bank_free[k])
                for q in range(n):
                    done = p_done.mark(pe.transpose(banks[:, k, q * D:(q + 1) * D], src_tile(t0 + q), ident[:, :]))
                eng, cnt = (dve, v_done) if (t0 // 4) % 2 else (act, a_done)
                wait(eng, done)
                o, s = out_block(t0, n), banks[:, k, 0:n * D]
                bank_free[k] = cnt.mark(eng.tensor_copy(o, s) if eng is dve else eng.copy(o, s))
                marks.append(bank_free[k])
            return marks[-2:]

        def T_to_N(src, out3, ready):
            return turn_tiles(lambda t: src[:, t * D:(t + 1) * D],
                              lambda t0, n: out3[:, t0:t0 + n, :].rearrange("p t f -> p (t f)"), ready)

        def N_to_T(src3, out_, ready):
            marks = turn_tiles(lambda t: src3[:, t, :], lambda t0, n: out_[:, t0 * D:(t0 + n) * D], ready)
            wait(dve, *marks)
            return [v_done.mark(dve.memset(out_[:, N_NODES:NP], 0.0))]

        def write_table(src3, table, ready):
            wait(sp, *ready)
            return table_w.mark(sp.dma_start(table.rearrange("(t p) f -> p t f", p=D), src3))

        def node_product(src, rhs, width, ready, bias=None):
            wait(pe, *ready)
            per = 512 // width
            marks = []
            for t0 in range(0, N_TILES, per):
                n = min(per, N_TILES - t0)
                k = bank()
                if bank_free[k]:
                    wait(pe, bank_free[k])
                for q in range(n):
                    mm = pe.matmul(banks[:, k, q * width:(q + 1) * width], src[:, (t0 + q) * D:(t0 + q + 1) * D], rhs,
                                   start=True, stop=True)
                done = p_done.mark(mm)
                eng, cnt = (dve, v_done) if (t0 // per) % 2 else (act, a_done)
                wait(eng, done)
                o = tN[:, t0:t0 + n, 0:width]
                s = banks[:, k, 0:n * width].rearrange("p (t f) -> p t f", f=width)
                bank_free[k] = cnt.mark(eng.tensor_copy(o, s) if eng is dve else eng.copy(o, s))
                marks.append(bank_free[k])
            return marks[-2:]

        def norm_N(v3, ready, tmp3):
            mean, var, std, inv = (vec[:, k * N_TILES:(k + 1) * N_TILES] for k in range(4))
            wait(dve, *ready)
            t = v_done.mark(dve.tensor_reduce(mean, v3, AX.X, ALU.add))
            wait(dve, t)
            t = v_done.mark(dve.tensor_scalar(mean, mean, 1.0 / D, None, ALU.mult))
            wait(dve, t)
            t = v_done.mark(dve.tensor_tensor(v3, v3, mean.unsqueeze(2).to_broadcast([D, N_TILES, D]), ALU.subtract))
            wait(act, t)
            t = a_done.mark(act.activation(tmp3, v3, ACT.Square))
            wait(dve, t)
            t = v_done.mark(dve.tensor_reduce(var, tmp3, AX.X, ALU.add))
            wait(act, t)
            t = a_done.mark(act.activation(std, var, ACT.Sqrt, bias=eps_c[:, :], scale=1.0 / D))
            wait(dve, t)
            t = v_done.mark(dve.reciprocal(inv, std))
            wait(dve, t)
            return v_done.mark(dve.tensor_tensor(v3, v3, inv.unsqueeze(2).to_broadcast([D, N_TILES, D]), ALU.mult))

        def add_and_norm(yT, ready):
            y3 = tN[:, :, 0:D]
            marks = T_to_N_wide(yT, ready)
            wait(dve, *marks)
            t = v_done.mark(dve.tensor_tensor(xN[:, :, :], xN[:, :, :], y3, ALU.add))
            return norm_N(xN[:, :, :], [t], y3)

        def T_to_N_wide(src, ready):
            wait(pe, *ready)
            marks = []
            for t0 in range(0, N_TILES, 4):
                n = min(4, N_TILES - t0)
                k = bank()
                if bank_free[k]:
                    wait(pe, bank_free[k])
                for q in range(n):
                    done = p_done.mark(pe.transpose(banks[:, k, q * D:(q + 1) * D],
                                                    src[:, (t0 + q) * D:(t0 + q + 1) * D], ident[:, :]))
                eng, cnt = (dve, v_done) if (t0 // 4) % 2 else (act, a_done)
                wait(eng, done)
                o, s = tN[:, t0:t0 + n, 0:D], banks[:, k, 0:n * D].rearrange("p (t f) -> p t f", f=D)
                bank_free[k] = cnt.mark(eng.tensor_copy(o, s) if eng is dve else eng.copy(o, s))
                marks.append(bank_free[k])
            return marks[-2:]

        one_eps = eps_sb
        wait(dve, *in_)
        one = v_done.mark(dve.tensor_scalar(one_eps[:, :], eps_sb[:, :], 1.0, None, ALU.add))

        def gin(layer, inT, wa, ba, g_, bt, wb, bb, func, summed):
            a0 = acc[:, 0, :]
            hid = acc[:, 1, :]
            c = chan
            wait(dve, summed, one)
            t = v_done.mark(dve.scalar_tensor_tensor(out=a0, in0=inT[:, :], scalar=one_eps[:, layer:layer + 1], in1=a0,
                                                     op0=ALU.mult, op1=ALU.add))
            t = product_T([(W(wa), a0)], [t], to_act(hid, ACT.Identity, col(ba)))
            wait(dve, t)
            t = v_done.mark(dve.tensor_reduce(c[:, 0:1], hid[:, 0:N_NODES], AX.X, ALU.add))
            wait(dve, t)
            t = v_done.mark(dve.tensor_scalar(c[:, 1:2], c[:, 0:1], -1.0 / N_NODES, None, ALU.mult))
            wait(act, t)
            t = a_done.mark(act.activation(a0[:, 0:N_NODES], hid[:, 0:N_NODES], ACT.Square, bias=c[:, 1:2],
                                           accum_out=c[:, 2:3]))
            wait(act, t)
            t = a_done.mark(act.activation(c[:, 3:4], c[:, 2:3], ACT.Sqrt, bias=eps_c[:, :], scale=1.0 / N_NODES))
            wait(dve, t)
            t = v_done.mark(dve.reciprocal(c[:, 4:5], c[:, 3:4]))
            wait(dve, t)
            t = v_done.mark(dve.tensor_tensor(c[:, 5:6], c[:, 4:5], col(g_), ALU.mult))
            wait(dve, t)
            t = v_done.mark(dve.scalar_tensor_tensor(out=c[:, 6:7], in0=c[:, 1:2], scalar=c[:, 5:6], in1=col(bt),
                                                     op0=ALU.mult, op1=ALU.add))
            wait(act, t)
            t = a_done.mark(act.activation(a0, hid, ACT.Relu, bias=c[:, 6:7], scale=c[:, 5:6]))
            return product_T([(W(wb), a0)], [t], to_act(tA, func, col(bb)))

        s = sum_neighbours(x_n, list(in_), with_degree=True)
        t = gin(0, xT, "w1a", "b1a", "g1", "bt1", "w1b", "b1b", ACT.Relu, s)
        m = T_to_N_wide(tA, [t])
        t1 = write_table(tN[:, :, 0:D], tab0, m)
        s = sum_neighbours(tab0, [t1])
        t = gin(1, tA, "w2a", "b2a", "g2", "bt2", "w2b", "b2b", ACT.Identity, s)
        xn_ready = add_and_norm(tA, [t])
        xt_ready = N_to_T(xN, xT, [xn_ready])

        def block1(xn_ready, xt_ready):
            m = node_product(xT, W("msg_xs"), D, xt_ready)
            t = write_table(tN[:, :, 0:D], tabs, m)
            wait(act, t)
            wait(dve, t)
            m = node_product(xT, W("msg_xd"), D, [])
            wait(dve, *m)
            bias = row("msg_b1").unsqueeze(1).to_broadcast([D, N_TILES, D])
            t = v_done.mark(dve.tensor_tensor(tN[:, :, 0:D], tN[:, :, 0:D], bias, ALU.add))
            t = write_table(tN[:, :, 0:D], tabd, [t])
            wait(dve, *clear_acc(1))
            wait(pool, t)
            wait(sp, sc_mm.now(), st_mm.now())

            def edge_product(i, j):
                g = i * UNROLL + j
                wait(pe, e_ready(i, j))
                wait(pe, (pre.sem, pre.n + g - 1))
                for c in range(GC):
                    mm = pe.matmul(banks[:, 2 * (j % 2), c * D:(c + 1) * D], e_ring[:, j % E_SLOTS, c * D:(c + 1) * D],
                                   W("msg_e"), start=True, stop=True)
                mm.then_inc(ve_mm.sem, 1)

            sums = [(acc[:, 0, :], D)]
            with nc.Fori(0, NG // UNROLL) as i:
                w0 = {}
                edge_product(i, 0)
                for j in range(UNROLL):
                    g = i * UNROLL + j
                    if j % W0_AHEAD == 0:
                        window_starts(i, j, w0)
                    load_idx(g, j, [src_g, dst_g], sc_mm)
                    load_e(g, j)
                    gather(i, j, [(tabs, 0, D), (tabd, D, D)], [(sc_mm.sem, sc_mm.n + g - (UNROLL - 1))])
                    wait(dve, rows_ready(i, j, tables=2))
                    wait(dve, (ve_mm.sem, ve_mm.n + g + 1))
                    a, b = m_ring[j][:, :, 0:D], m_ring[j][:, :, D:2 * D]
                    dve.tensor_tensor(a, a, banks[:, 2 * (j % 2), :].rearrange("p (c f) -> p c f", f=D),
                                      ALU.add).then_inc(msg.sem, 1)
                    wait(dve, (msg.sem, msg.n + g + 1))
                    dve.tensor_tensor(a, a, b, ALU.add).then_inc(pre.sem, 1)
                    wide_add(g, sums)
                    one_hot(g, j)
                    if j:
                        segment_add(g - 1, w0[j - 1], sc_mm, acc_ps[:, (j - 1) % 2, :], sums)
                    wait(act, (pre.sem, pre.n + g + 1))
                    act.activation(a, a, ACT.Silu).then_inc(sq.sem, 1)
                    if j + 1 < UNROLL:
                        edge_product(i, j + 1)
                    segment_mm(g, j, [(sq.sem, sq.n + g + 1)], [(lambda c, j=j: m_ring[j][:, c, 0:D], D)])
                segment_add(g, w0[j], sc_mm, acc_ps[:, j % 2, :], sums)
            rings_counted(idx=2, e=1, rows=2)
            for c in (ve_mm, pre, msg, sq):
                c.n += NG
            segments_counted()
            for k in range(4):
                bank_free[k] = pre.now()

            a0, a1 = acc[:, 0, :], acc[:, 1, :]
            t = product_T([(W("msg_2"), a0), (row("msg_b2")[0:1, :], deg)], [sc_add.now()], to_act(a1, ACT.Identity, 0.0))
            t = product_T([(W("upd_x"), xT), (W("upd_a"), a1)], [t, *xt_ready], to_act(a0, ACT.Silu, col("upd_b1")))
            t = product_T([(W("upd_2"), a0)], [t], to_act(tA, ACT.Identity, col("upd_b2")))
            y3 = tN[:, :, 0:D]
            m = T_to_N_wide(tA, [t])
            wait(dve, *m)
            t = v_done.mark(dve.tensor_tensor(y3, y3, xN[:, :, :], ALU.add))
            t = norm_N(y3, [t], tN[:, :, D:2 * D])
            wait(dve, t)
            t = v_done.mark(dve.tensor_tensor(y3, y3, row("ln_g").unsqueeze(1).to_broadcast([D, N_TILES, D]), ALU.mult))
            wait(dve, t)
            t = v_done.mark(dve.tensor_tensor(y3, y3, row("ln_b").unsqueeze(1).to_broadcast([D, N_TILES, D]), ALU.add))
            wait(dve, t)
            t = v_done.mark(dve.tensor_tensor(xN[:, :, :], xN[:, :, :], y3, ALU.add))
            xn = norm_N(xN[:, :, :], [t], y3)
            return xn, N_to_T(xN, xT, [xn])

        def block2(xn_ready, xt_ready):
            hT, h_ready = xT, list(xt_ready)
            for l in range(N_LAYERS2):
                c = chan
                SG, AB, B1, MEAN, EX2, VAR, S, SH, LOW = (c[:, 2 * k:2 * k + 2] for k in range(9))
                gam, bet, b1 = (col_all[:, COLS.index(f"{k}{l}0"):COLS.index(f"{k}{l}0") + 2] for k in ("g", "bt", "b"))
                t = v_done.mark(dve.tensor_scalar(SG, gam, 0.0, 2.0, ALU.is_ge, ALU.mult))
                wait(dve, t)
                t = v_done.mark(dve.tensor_scalar(SG, SG, -1.0, None, ALU.add))
                wait(dve, t)
                v_done.mark(dve.tensor_tensor(B1, SG, b1, ALU.mult))
                t = v_done.mark(dve.tensor_tensor(AB, SG, gam, ALU.mult))
                wait(dve, t)
                t = v_done.mark(dve.tensor_scalar(AB, AB, TINY, None, ALU.max))

                def spread(cols2, dst, t):
                    for h in range(2):
                        wait(dve, t)
                        t = v_done.mark(dve.tensor_scalar(diag[:, :], ident[:, :], cols2[:, h:h + 1], None, ALU.mult))
                        wait(pe, t)
                        t = p_done.mark(pe.matmul(x_ps[:, 0:D], ones[:, :], diag[:, :], start=True, stop=True))
                        wait(dve, t)
                        t = v_done.mark(dve.tensor_copy(dst[:, h * D:(h + 1) * D], x_ps[:, 0:D]))
                    return t

                t = spread(SG, sgn, t)
                wait(dve, t)
                v_done.mark(dve.tensor_tensor(W(f"eh{l}"), W(f"eh{l}"), sgn[:, :], ALU.mult))
                t = v_done.mark(dve.tensor_tensor(W(f"ee{l}"), W(f"ee{l}"), sgn[:, :], ALU.mult))
                m = node_product(hT, W(f"eh{l}"), 2 * D, [t] + h_ready)
                t = write_table(tN[:, :, :], tab2, m)
                wait(pool, t)
                wait(sp, sc_mm.now(), st_mm.now())
                zero = small[:, 8:9]
                sq_acc = acc[:, 0, 0:GC * 2 * D]
                v_done.mark(dve.memset(sq_acc, 0.0))
                t = v_done.mark(dve.memset(zero, 0.0))
                wait(pe, t)
                wait(dve, t)
                pe.matmul(st_ps[0:1, :], zero, node_no[:, 0:512], start=True, stop=False, skip_group_check=True)

                def relu_e(i, j):
                    if l:
                        hold(act, e_ready(i, j))
                        e = e_ring[:, j % E_SLOTS, :]
                        act.activation(e, e, ACT.Relu).then_inc(e_relu.sem, 1)

                def edge_product(i, j):
                    g = i * UNROLL + j
                    wait(pe, (e_relu.sem, e_relu.n + g + 1) if l else e_ready(i, j))
                    wait(pe, (pre.sem, pre.n + g - 1))
                    for c_ in range(GC):
                        mm = pe.matmul(banks[:, 2 * (j % 2) + c_ // 2, (c_ % 2) * 256:(c_ % 2) * 256 + 256],
                                       e_ring[:, j % E_SLOTS, c_ * D:(c_ + 1) * D], W(f"ee{l}"), start=True, stop=True)
                    mm.then_inc(ve_mm.sem, 1)

                def add_squares(g, j):
                    wait(dve, (sq.sem, sq.n + g + 1))
                    wait(dve, (sq_add.sem, sq_add.n + g))
                    dve.tensor_tensor(sq_acc, sq_acc, sq_ring[:, j % 2, :], ALU.add).then_inc(sq_add.sem, 1)

                with nc.Fori(0, NG // UNROLL) as i:
                    relu_e(i, 0)
                    edge_product(i, 0)
                    for j in range(UNROLL):
                        g = i * UNROLL + j
                        load_idx(g, j, [src_g], st_mm)
                        load_e(g, j)
                        gather(i, j, [(tab2, 0, 2 * D)],
                               [(st_mm.sem, st_mm.n + g - (UNROLL - 1)), (sq.sem, sq.n + g - (UNROLL - 1)),
                                (pre_out[j].sem, pre_out[j].n + 16 * i)])
                        wait(dve, rows_ready(i, j))
                        wait(dve, (ve_mm.sem, ve_mm.n + g + 1))
                        p = m_ring[j].rearrange("p c f -> p (c f)")
                        v = banks[:, 2 * (j % 2):2 * (j % 2) + 2, :].rearrange("p b f -> p (b f)")
                        dve.tensor_tensor(p, p, v, ALU.add).then_inc(pre.sem, 1)
                        if j:
                            add_squares(g - 1, j - 1)
                        if j + 1 < UNROLL:
                            relu_e(i, j + 1)
                            edge_product(i, j + 1)
                        hold(act, (pre.sem, pre.n + g + 1))
                        act.dma_start(pre_dram[bass.ds(g, 1), :, :].rearrange("a p k -> (a p) k"), p
                                      ).then_inc(pre_out[j].sem, 16)
                        wait(act, (sq_add.sem, sq_add.n + g - 1))
                        act.activation(sq_ring[:, j % 2, :], p, ACT.Square).then_inc(sq.sem, 1)
                        wait(pe, (pre.sem, pre.n + g + 1))
                        for h in range(2):
                            mm = pe.matmul(st_ps[0:1, :], ones[:, 0:1], p[:, h * 512:(h + 1) * 512],
                                           start=False, stop=False, skip_group_check=True)
                        mm.then_inc(st_mm.sem, 1)
                    add_squares(g, j)
                rings_counted(idx=1, e=1, rows=1, pre_o=1)
                for q in (ve_mm, pre, sq, st_mm, sq_add) + ((e_relu,) if l else ()):
                    q.n += NG
                for k in range(4):
                    bank_free[k] = pre.now()

                wait(dve, st_mm.now())
                t = v_done.mark(dve.tensor_copy(sums_row[:, :], st_ps[0:1, :]))
                wait(pe, t, sq_add.now())
                for h in range(2):
                    for k in range(2):
                        pe.matmul(x_ps[:, h:h + 1], sums_row[0:1, k * 256 + h * D:k * 256 + (h + 1) * D],
                                  ones[0:1, 0:1], start=(k == 0), stop=(k == 1))
                    for k in range(GC):
                        mm = pe.matmul(x_ps[:, 2 + h:3 + h], sq_acc[:, k * 256 + h * D:k * 256 + (h + 1) * D],
                                       ones[:, 0:1], start=(k == 0), stop=(k == GC - 1))
                t = p_done.mark(mm)

                wait(dve, t)
                v_done.mark(dve.tensor_scalar(MEAN, x_ps[:, 0:2], 1.0 / N_EDGES, None, ALU.mult))
                t = v_done.mark(dve.tensor_scalar(EX2, x_ps[:, 2:4], 1.0 / N_EDGES, None, ALU.mult))
                wait(dve, t)
                t = v_done.mark(dve.tensor_tensor(VAR, MEAN, MEAN, ALU.mult))
                wait(dve, t)
                t = v_done.mark(dve.tensor_tensor(VAR, EX2, VAR, ALU.subtract))
                wait(dve, t)
                t = v_done.mark(dve.tensor_scalar(VAR, VAR, 0.0, None, ALU.max))
                wait(act, t)
                t = a_done.mark(act.activation(S, VAR, ACT.Sqrt, bias=eps_c[:, :]))
                wait(dve, t)
                t = v_done.mark(dve.reciprocal(S, S))
                t = v_done.mark(dve.tensor_tensor(MEAN, MEAN, B1, ALU.add))
                wait(dve, t)
                t = v_done.mark(dve.tensor_tensor(SH, B1, MEAN, ALU.subtract))
                wait(dve, t)
                t = v_done.mark(dve.tensor_tensor(S, S, AB, ALU.mult))
                wait(dve, t)
                t = v_done.mark(dve.reciprocal(LOW, S))
                wait(dve, t)
                t = v_done.mark(dve.tensor_tensor(LOW, LOW, bet, ALU.mult))
                wait(dve, t)
                t = v_done.mark(dve.tensor_tensor(LOW, LOW, SH, ALU.add))
                wait(dve, t)
                t = v_done.mark(dve.tensor_scalar(LOW, LOW, -1.0, None, ALU.mult))
                v_done.mark(dve.tensor_tensor(SH, SH, S, ALU.mult))
                wait(dve, v_done.now())
                v_done.mark(dve.tensor_tensor(SH, SH, bet, ALU.add))
                t = spread(LOW, low, v_done.now())

                wait(dve, t, *clear_acc(2))
                wait(sp, *[q.now() for q in pre_out], st_mm.now(), sq.now(), sc_mm.now())
                sums = [(acc[:, 0, :], D), (acc[:, 1, :], D)]

                def transpose_window(g, j):
                    wait(pe, (win_out.sem, win_out.n + g + 1))
                    hold(pe, (sc_add.sem, sc_add.n + g - 1))
                    for h in range(2):
                        mm = pe.transpose(banks[:, j % 2, h * WIN:(h + 1) * WIN],
                                          win_ring[:, j % 2, h * D:(h + 1) * D], ident[0:WIN, 0:WIN])
                    mm.then_inc(win_t.sem, 1)

                with nc.Fori(0, NG // UNROLL) as i:
                    w0 = {}
                    for j in range(UNROLL):
                        g = i * UNROLL + j
                        p = m_ring[j]
                        if j % W0_AHEAD == 0:
                            window_starts(i, j, w0)
                        hold(sp, (sc_mm.sem, sc_mm.n + g - (UNROLL - 1)))
                        sp.dma_start(p.rearrange("p c f -> p (c f)"),
                                     pre_dram[bass.ds(g, 1), :, :].rearrange("a p k -> (a p) k")
                                     ).then_inc(pre_in[j].sem, 16)
                        wait(dve, (pre_in[j].sem, pre_in[j].n + 16 * (i + 1)))
                        dve.tensor_tensor(p, p, low[:, :].unsqueeze(1).to_broadcast([D, GC, 2 * D]), ALU.max
                                          ).then_inc(msg.sem, 1)
                        wide_add(g, sums)
                        one_hot(g, j)
                        if j >= 2:
                            segment_add(g - 2, w0[j - 2], win_t, banks[:, j % 2, :], sums)
                        wait(pe, (msg.sem, msg.n + g + 1))
                        wide_mm(g, [(lambda c_, j=j: m_ring[j][:, c_, 0:D], D),
                                    (lambda c_, j=j: m_ring[j][:, c_, D:2 * D], D)])
                        wait(pe, (oh.sem, oh.n + g + 1))
                        wait(pe, (win_out.sem, win_out.n + g - 1))
                        for c_ in range(GC):
                            mm = pe.matmul(acc_ps[0:WIN, j % 2, 0:2 * D], oh_ring[:, j % 2, c_, :], m_ring[j][:, c_, :],
                                           start=(c_ == 0), stop=(c_ == GC - 1))
                        mm.then_inc(sc_mm.sem, 1)
                        if j:
                            transpose_window(g - 1, j - 1)
                        wait(act, (sc_mm.sem, sc_mm.n + g + 1))
                        wait(act, (win_t.sem, win_t.n + g - 1))
                        act.copy(win_ring[:, j % 2, :], acc_ps[0:WIN, j % 2, 0:2 * D]).then_inc(win_out.sem, 1)
                    transpose_window(g, j)
                    for k in (1, 0):
                        segment_add(g - k, w0[j - k], win_t, banks[:, (j - k) % 2, :], sums)
                rings_counted(pre_i=1)
                for q in (msg, win_out, win_t):
                    q.n += NG
                segments_counted()
                for k in range(4):
                    bank_free[k] = sc_add.now()

                wait(pe, v_done.now(), sc_add.now())
                pe.matmul(x_ps[0:1, 0:D], SH[:, 0:1], W(f"eo_lo{l}"), start=True, stop=False)
                t = p_done.mark(pe.matmul(x_ps[0:1, 0:D], SH[:, 1:2], W(f"eo_hi{l}"), start=False, stop=True))
                wait(dve, t)
                v_done.mark(dve.tensor_tensor(v_row[:, :], x_ps[0:1, 0:D], row(f"eo_b{l}")[0:1, :], ALU.add))
                v_done.mark(dve.tensor_scalar(W(f"eo_lo{l}"), W(f"eo_lo{l}"), S[:, 0:1], None, ALU.mult))
                t = v_done.mark(dve.tensor_scalar(W(f"eo_hi{l}"), W(f"eo_hi{l}"), S[:, 1:2], None, ALU.mult))
                func = ACT.Relu if l < N_LAYERS2 - 1 else ACT.Identity
                t = product_T([(W(f"eo_lo{l}"), acc[:, 0, :]), (W(f"eo_hi{l}"), acc[:, 1, :]), (v_row[:, :], deg)],
                              [t, sc_add.now()], to_act(tA, func, 0.0))
                hT, h_ready = tA, [t]
                wait(dve, t)
            xn = add_and_norm(tA, h_ready)
            return xn, None

        def block3(xn_ready):
            t = write_table(xN[:, :, :], tab0, [xn_ready])
            for layer, (w, b) in enumerate((("sage1", "sage_b1"), ("sage2", "sage_b2"))):
                s = sum_neighbours(tab0, [t])
                t = product_T([(W(w), acc[:, 0, :])], [s], to_act(tA, ACT.Relu, col(b)))
                if layer == 0:
                    m = T_to_N_wide(tA, [t])
                    t = write_table(tN[:, :, 0:D], tab0, m)
            return add_and_norm(tA, [t])

        stages = [lambda: None]
        if stop_at is None or stop_at > 1:
            xn_ready, xt_ready = block1(xn_ready, xt_ready)
        if stop_at is None or stop_at > 2:
            xn_ready, _ = block2(xn_ready, xt_ready)
        if stop_at is None or stop_at > 3:
            xn_ready = block3(xn_ready)

        wait(sp, xn_ready)
        full = N_NODES // D
        out_w.mark(sp.dma_start(out[0:full * D, :].rearrange("(t p) f -> p t f", p=D), xN[:, 0:full, :]))
        out_w.mark(sp.dma_start(out[full * D:N_NODES, :], xN[0:N_NODES - full * D, full, :]))
        wait(sp, out_w.now(), table_w.now(), *[q.now() for q in pre_out])


WIDE_FROM = WIN


def kernel(**inputs):
    import numpy as np
    import concourse.bacc as bacc
    from concourse.bass_utils import run_bass_kernel_spmd

    a = {k: np.asarray(v) for k, v in inputs.items()}

    def padded(v, shape, fill):
        o = np.full(shape, fill, v.dtype)
        o[tuple(slice(0, n) for n in v.shape)] = v
        return o

    x = padded(a["x"], (NP, D), 0)
    src = padded(a["src"], (EP,), NP - 1).reshape(NG, GC, D)
    dst = padded(a["dst"], (EP,), -1).reshape(NG, GC, D)
    dst_ok = padded(a["dst"], (EP,), NP - 1).reshape(NG, GC, D)
    w = {"w1a": a["L0_gnn_w1a"], "w1b": a["L0_gnn_w1b"], "w2a": a["L0_gnn_w2a"], "w2b": a["L0_gnn_w2b"],
         "msg_xs": a["L1_gnn_msg_W1"][0:D], "msg_xd": a["L1_gnn_msg_W1"][D:2 * D], "msg_e": a["L1_gnn_msg_W1"][2 * D:],
         "msg_2": a["L1_gnn_msg_W2"], "upd_x": a["L1_gnn_upd_W1"][0:D], "upd_a": a["L1_gnn_upd_W1"][D:],
         "upd_2": a["L1_gnn_upd_W2"], "sage1": a["L3_gnn_W1"].T, "sage2": a["L3_gnn_W2"].T}
    c = {"b1a": a["L0_gnn_b1a"], "g1": a["L0_gnn_g1"], "bt1": a["L0_gnn_bt1"], "b1b": a["L0_gnn_b1b"],
         "b2a": a["L0_gnn_b2a"], "g2": a["L0_gnn_g2"], "bt2": a["L0_gnn_bt2"], "b2b": a["L0_gnn_b2b"],
         "upd_b1": a["L1_gnn_upd_b1"], "upd_b2": a["L1_gnn_upd_b2"], "sage_b1": a["L3_gnn_b1"], "sage_b2": a["L3_gnn_b2"]}
    r = {"msg_b1": a["L1_gnn_msg_b1"], "msg_b2": a["L1_gnn_msg_b2"], "ln_g": a["L1_gnn_ln_gamma"],
         "ln_b": a["L1_gnn_ln_beta"]}
    for l in range(N_LAYERS2):
        w1, w2 = a["L2_gnn_W1"][l].T, a["L2_gnn_W2"][l].T
        w |= {f"eh{l}": w1[0:D], f"ee{l}": w1[D:], f"eo_lo{l}": w2[0:D], f"eo_hi{l}": w2[D:]}
        for h in range(2):
            part = slice(h * D, (h + 1) * D)
            c |= {f"b{l}{h}": a["L2_gnn_b1"][l][part], f"g{l}{h}": a["L2_gnn_gamma"][l][part],
                  f"bt{l}{h}": a["L2_gnn_beta"][l][part]}
        r[f"eo_b{l}"] = a["L2_gnn_b2"][l]
    arrays = {
        "x_n": x, "x_t": x.T, "e_t": padded(a["edge_attr_128"], (EP, D), 0).T,
        "src_g": src.transpose(0, 2, 1), "dst_g": dst_ok.transpose(0, 2, 1),
        "dst_p": dst.reshape(NG * GC, D).T,
        "weights": np.concatenate([w[k] for k in WEIGHTS], axis=1),
        "cols": np.stack([c[k] for k in COLS], axis=1), "rows": np.stack([r[k] for k in ROWS]),
        "eps": np.stack([a["L0_gnn_eps1"], a["L0_gnn_eps2"]]).reshape(1, 2),
    }
    arrays = {k: np.ascontiguousarray(v) for k, v in arrays.items()}
    nc = bacc.Bacc("TRN2", target_bir_lowering=False, num_devices=1)
    args = [nc.dram_tensor(k, v.shape, mybir.dt.from_np(v.dtype), kind="ExternalInput").ap() for k, v in arrays.items()]
    o = nc.dram_tensor("out", (N_NODES, D), F32, kind="ExternalOutput").ap()
    build(nc, *args, o)
    return run_bass_kernel_spmd(nc, [arrays], core_ids=[0]).results[0]["out"]
```

```python
from contextlib import ExitStack

import concourse.bass as bass
from concourse import mybir

F32 = mybir.dt.float32
I32 = mybir.dt.int32
BF16 = mybir.dt.bfloat16
FP16 = mybir.dt.float16
ALU = mybir.AluOpType
ACT = mybir.ActivationFunctionType
AX = mybir.AxisListType

D = 128
N_NODES = 3125
N_TILES = -(-N_NODES // D)
NP = N_TILES * D
N_EDGES = 53125
GC = 4
GE = GC * D
NG = -(-N_EDGES // GE)
EP = NG * GE
WIN = 64
N_WIN = NP // WIN
UNROLL = 8
E_SLOTS = 4
OH_SLOTS = 4
ADJ_WIN = 40
ADJ_BLOCK = 320
MAX_COUNT = 256
LAG = 2
EPS = 1e-5
TINY = 1e-30
N_LAYERS2 = 3

WEIGHTS, _at = {}, 0
for _n, _w in ([("w1a", 1), ("w1b", 1), ("w2a", 1), ("w2b", 1), ("msg_xs", 1), ("msg_xd", 1), ("msg_e", 1),
                ("msg_2", 1), ("upd_x", 1), ("upd_a", 1), ("upd_2", 1), ("sage1", 1), ("sage2", 1)]
               + [(f"{k}{l}", w) for l in range(N_LAYERS2) for k, w in
                  (("eh", 2), ("ee", 2), ("eo_lo", 1), ("eo_hi", 1))]):
    WEIGHTS[_n] = (_at, _w * D)
    _at += _w * D
W_COLS = _at
COLS = ["b1a", "g1", "bt1", "b1b", "b2a", "g2", "bt2", "b2b", "upd_b1", "upd_b2", "sage_b1", "sage_b2"] + [
    f"{k}{l}{h}" for l in range(N_LAYERS2) for k in ("b", "g", "bt") for h in (0, 1)]
ROWS = ["msg_b1", "msg_b2", "ln_g", "ln_b"] + [f"eo_b{l}" for l in range(N_LAYERS2)]


class Count:

    def __init__(self, sem, by=1):
        self.sem, self.by, self.n = sem, by, 0

    def mark(self, ins):
        ins.then_inc(self.sem, self.by)
        self.n += self.by
        return (self.sem, self.n)

    def now(self):
        return (self.sem, self.n)


def wait(eng, *marks):
    for sem, value in marks:
        eng.wait_ge(sem, value)


def hold(eng, *marks):
    for mark in marks:
        wait(eng, mark)
        eng.nop(nofuse=True)


def build(nc, x_n, x_t, e_t, src_g, dst_g, dst_p, dst_row, src_p, weights, cols, rows, eps, out):
    pe, dve, act, pool, sp = nc.tensor, nc.vector, nc.scalar, nc.gpsimd, nc.sync
    with ExitStack() as ctx:
        def sb(name, shape, dt=F32):
            return ctx.enter_context(nc.sbuf_tensor(name, shape, dt))

        def sem(name):
            return ctx.enter_context(nc.semaphore(name))

        def dram(name, shape, dt=F32):
            return nc.dram_tensor(name, shape, dt, kind="Internal").ap()

        w_all = sb("w_all", [D, W_COLS])
        col_all = sb("col_all", [D, len(COLS)])
        row_all = sb("row_all", [D, len(ROWS) * D])
        one_eps = sb("one_eps", [D, 2])
        ident = sb("ident", [D, D])
        ones = sb("ones", [D, D])
        eps_c = sb("eps_c", [D, 1])
        node_no = sb("node_no", [D, NP])
        node_col_i = sb("node_col_i", [WIN, 1], I32)
        dst_i = sb("dst_i", [D, NG * GC], I32)
        dst_rel = sb("dst_rel", [D, NG * GC])
        w0_i = sb("w0_i", [1, LAG + NG], I32)
        any_wide = sb("any_wide", [1, 1], I32)
        small = sb("small", [D, 64])
        diag = sb("diag", [D, D])
        xT = sb("xT", [D, NP])
        xN = sb("xN", [D, N_TILES, D])
        acc = sb("acc", [D, 2, NP])
        deg = sb("deg", [1, NP])
        tA = sb("tA", [D, NP])
        tN = sb("tN", [D, N_TILES, 2 * D])
        vec = sb("vec", [D, 4 * N_TILES])
        m_half = sb("m_half", [D, UNROLL // 2, GC, 2 * D])
        e_ring = sb("e_ring", [D, E_SLOTS, GE])
        idx_ring = sb("idx_ring", [D, UNROLL, 2, GC], I32)
        oh_ring = sb("oh_ring", [D, OH_SLOTS, GC, WIN])
        oh_wide = sb("oh_wide", [D, GC, WIN])
        sq_ring = sb("sq_ring", [D, 2, GC * 2 * D])
        key = sb("key", [D, NG * GC])
        lane = sb("lane", [D, NG * GC])
        adj_at = sb("adj_at", [D, NG])
        adj_at_i = sb("adj_at_i", [1, NG], I32)
        carry_i = sb("carry_i", [1, NG], I32)
        irregular = sb("irregular", [1, 1], I32)
        key_no = sb("key_no", [D, ADJ_WIN * N_TILES], FP16)
        ident_bf = sb("ident_bf", [D, D], BF16)
        lane_ring = sb("lane_ring", [D, 2, GC, D], BF16)
        adj_ring = sb("adj_ring", [D, 2, ADJ_WIN * N_TILES], BF16)
        dst_ring = sb("dst_ring", [WIN, E_SLOTS, GE], I32)
        tabd_ring = sb("tabd_ring", [WIN, E_SLOTS, D])
        ohT_ring = sb("ohT_ring", [WIN, 2, GE])
        win_node = sb("win_node", [WIN, NG])
        win_ring = sb("win_ring", [WIN, 2, 2 * D])
        sums_row = sb("sums_row", [1, 512])
        low = sb("low", [D, 2 * D])
        sgn = low
        v_row = sb("v_row", [1, D])
        chan = sb("chan", [D, 32])

        banks = ctx.enter_context(nc.psum_tensor("banks", [D, 4, 512], F32))
        acc_ps = ctx.enter_context(nc.psum_tensor("acc_ps", [D, 2, 512], F32))
        st_ps = ctx.enter_context(nc.psum_tensor("st_ps", [D, 512], F32))
        x_ps = ctx.enter_context(nc.psum_tensor("x_ps", [D, 512], F32))

        tab0 = dram("tab0", [NP, D])
        tabs = dram("tabs", [NP, D])
        tabd = dram("tabd", [NP, D])
        tab2 = dram("tab2", [NP, 2 * D])
        pre_dram = dram("pre_dram", [NG, D, GC * 2 * D])

        adj = dram("adj", [D, NP, N_TILES], BF16)

        def as_bf16(tile, size):
            return tile.bitcast(BF16)[:, 0:size]

        key_ring = [as_bf16(r, GC * ADJ_WIN * N_TILES).rearrange("p (c k) -> p c k", c=GC)
                    for r in (e_ring.rearrange("p s e -> p (s e)"), sq_ring.rearrange("p s e -> p (s e)"))]
        adj_in = [as_bf16(r, ADJ_BLOCK * N_TILES).rearrange("p (d t) -> p d t", t=N_TILES)
                  for r in (m_half.rearrange("p j c f -> p (j c f)"), tN.rearrange("p t f -> p (t f)"))]
        parts = [as_bf16(acc[:, 1, 0:NP // 2], NP), as_bf16(acc[:, 1, NP // 2:NP], NP),
                 as_bf16(e_ring.rearrange("p s e -> p (s e)"), NP)]
        parts = [r.rearrange("p (t f) -> p t f", f=D) for r in parts]

        m_ring = [m_half[:, j, :, :] for j in range(UNROLL // 2)] + [
            tN[:, j * GC:(j + 1) * GC, :] for j in range(UNROLL // 2)]

        v_done, a_done, p_done, g_done = (Count(sem(s)) for s in ("v_done", "a_done", "p_done", "g_done"))
        loaded = Count(sem("loaded"), 16)
        table_w = Count(sem("table_w"), 16)
        table_again = Count(sem("table_again"), 16)
        out_w = Count(sem("out_w"), 16)
        idx_in = [Count(sem(f"idx_in{j}"), 16) for j in range(UNROLL)]
        e_in = [Count(sem(f"e_in{j}"), 16) for j in range(E_SLOTS)]
        rows_in = [Count(sem(f"rows_in{j}"), 16) for j in range(UNROLL)]
        rows_again = [Count(sem(f"rows_again{j}"), 16) for j in range(UNROLL)]
        pre_in = [Count(sem(f"pre_in{j}"), 16) for j in range(UNROLL)]
        pre_out = [Count(sem(f"pre_out{j}"), 16) for j in range(UNROLL)]
        e_relu = Count(sem("e_relu"))
        ve_mm = Count(sem("ve_mm"))
        pre = Count(sem("pre"))
        msg = Count(sem("msg"))
        sq = Count(sem("sq"))
        st_mm = Count(sem("st_mm"))
        sq_add = Count(sem("sq_add"))
        win_out = Count(sem("win_out"))
        win_t = Count(sem("win_t"))
        oh = Count(sem("oh"))
        ohT = Count(sem("ohT"))
        rows_x = [Count(sem(f"rows_x{j}"), 16) for j in range(UNROLL)]
        pre_x = Count(sem("pre_x"))
        key_oh = Count(sem("key_oh"))
        adj_mm = Count(sem("adj_mm"))
        adj_cp = Count(sem("adj_cp"))
        adj_st = Count(sem("adj_st"), 16)
        block_in = [Count(sem(f"block_in{k}"), 16) for k in range(2)]
        block_mm = Count(sem("block_mm"))
        block_out = Count(sem("block_out"))
        cleared = Count(sem("cleared"))
        sc_mm = Count(sem("sc_mm"))
        sc_add = Count(sem("sc_add"))
        oh_x, mm_x, add_x = (Count(sem(s)) for s in ("oh_x", "mm_x", "add_x"))

        def W(name):
            at, width = WEIGHTS[name]
            return w_all[:, at:at + width]

        def col(name):
            i = COLS.index(name)
            return col_all[:, i:i + 1]

        def row(name):
            i = ROWS.index(name)
            return row_all[:, i * D:(i + 1) * D]

        for q, (c, k) in enumerate(((sc_mm, UNROLL), (st_mm, UNROLL), (sq, UNROLL), (ve_mm, E_SLOTS), (ohT, E_SLOTS),
                                    (pre, 2), (sc_add, 2), (sq_add, 2), (adj_mm, 2), (adj_cp, 2), (block_mm, 2),
                                    (block_out, 2), (win_out, 2), (win_t, 2))):
            pool.memset(small[:, 16 + q:17 + q], 0.0).then_inc(c.sem, k)
            c.n = k
        g_done.mark(pool.memset(small[:, 0:1], 0.0))

        for dst, src in ((dst_i[:, :], dst_p), (xN[:, :, :], x_n.rearrange("(t p) f -> p t f", p=D)),
                         (row_all[:, :], rows.partition_broadcast(D).rearrange("p a f -> p (a f)")),
                         (one_eps[:, :], eps.partition_broadcast(D).rearrange("p a f -> p (a f)"))):
            loaded.mark(sp.dma_start(dst, src))
        src_i = tA[:, 1024:1024 + NG * GC].bitcast(I32)
        ins = [(xT[:, :], x_t), (col_all[:, :], cols)] + [
            (w_all[:, k * W_COLS // 6:(k + 1) * W_COLS // 6], weights[:, k * W_COLS // 6:(k + 1) * W_COLS // 6])
            for k in range(6)]
        for q, (dst, src) in zip(pre_out, ins):
            q.mark(act.dma_start(dst, src))
        loaded.mark(sp.dma_start(src_i, src_p))
        in_ = (loaded.now(), *[q.now() for q in pre_out])
        wait(pool, g_done.now())
        node_no_i = acc[:, 0, :].bitcast(I32)
        g_done.mark(pool.iota(node_no_i, [[1, NP]], base=0, channel_multiplier=0))
        g_done.mark(pool.iota(node_col_i[:, :], [[1, 1]], base=0, channel_multiplier=1))
        g_done.mark(pool.memset(ones[:, :], 1.0))
        g_done.mark(pool.memset(eps_c[:, :], EPS))
        z = g_done.mark(pool.memset(ident[:, :], 0.0))
        wait(pool, z)
        consts = g_done.mark(pool.affine_select(out=ident[:, :], in_=ident[:, :], compare_op=ALU.not_equal, fill=1.0,
                                                base=0, pattern=[[-1, D]], channel_multiplier=1))
        wait(dve, consts)
        v_done.mark(dve.tensor_copy(node_no[:, :], node_no_i))
        v_done.mark(dve.memset(deg[:, :], 0.0))

        wait(dve, *in_)
        t = v_done.mark(dve.tensor_copy(dst_rel[:, :], dst_i[:, :]))
        wait(dve, t)
        big = tA[:, 0:NG * GC]
        t = v_done.mark(dve.tensor_scalar(big, dst_rel[:, :], 0.0, 2.0 * NP, ALU.is_lt, ALU.mult))
        wait(dve, t)
        t = v_done.mark(dve.tensor_tensor(big, big, dst_rel[:, :], ALU.add))
        wait(dve, t)
        gmm = tA[:, 512:512 + 2 * NG]
        v_done.mark(dve.tensor_reduce(gmm[:, 0:NG], big.rearrange("p (g k) -> p g k", k=GC), AX.X, ALU.min))
        t = v_done.mark(dve.tensor_reduce(gmm[:, NG:2 * NG], dst_rel[:, :].rearrange("p (g k) -> p g k", k=GC),
                                          AX.X, ALU.max))
        top_diag = tA[0:NG, 3072:3072 + NG]
        carry_f = tA[0:1, 2048 - NG:2048]
        lane_f = tA[:, 1440:1440 + NG * GC]
        wait(pe, t, consts)
        for h in range(2):
            t = p_done.mark(pe.transpose(x_ps[0:NG, h * D:(h + 1) * D], gmm[:, h * NG:(h + 1) * NG], ident[:, :]))
        wait(dve, t)
        v_done.mark(dve.tensor_reduce(small[0:NG, 1:2], x_ps[0:NG, 0:D], AX.X, ALU.min))
        t = v_done.mark(dve.tensor_reduce(small[0:NG, 2:3], x_ps[0:NG, D:2 * D], AX.X, ALU.max))
        wait(dve, t)
        t = v_done.mark(dve.tensor_tensor(small[0:NG, 3:4], small[0:NG, 2:3], small[0:NG, 1:2], ALU.subtract))
        wait(dve, t)
        t = v_done.mark(dve.tensor_scalar(small[0:NG, 4:5], small[0:NG, 3:4], float(WIDE_FROM), None, ALU.is_ge))
        wait(pe, t)
        t = p_done.mark(pe.matmul(x_ps[:, 256:257], ones[0:NG, :], small[0:NG, 4:5], start=True, stop=True))
        wait(dve, t)
        v_done.mark(dve.tensor_copy(any_wide[:, :], x_ps[0:1, 256:257]))
        far = small[0:WIN, 11:12]
        v_done.mark(dve.tensor_copy(far, x_ps[0:WIN, 256:257]))
        part_no = v_done.mark(dve.tensor_copy(small[0:WIN, 10:11], node_col_i[:, :]))
        t = v_done.mark(dve.tensor_scalar(small[0:NG, 5:6], x_ps[0:NG, 256:257], 0.0, None, ALU.is_equal))
        wait(dve, t)
        t = v_done.mark(dve.tensor_tensor(small[0:NG, 6:7], small[0:NG, 5:6], small[0:NG, 1:2], ALU.mult))
        wait(dve, t)
        v_done.mark(dve.tensor_scalar(diag[0:NG, 0:NG], ident[0:NG, 0:NG], small[0:NG, 6:7], None, ALU.mult))
        t = v_done.mark(dve.tensor_scalar(top_diag, ident[0:NG, 0:NG], small[0:NG, 2:3], None, ALU.mult))
        wait(pe, t)
        pe.matmul(x_ps[:, 0:NG], ones[0:NG, :], diag[0:NG, 0:NG], start=True, stop=True)
        t = p_done.mark(pe.matmul(x_ps[:, 128:128 + NG], ones[0:NG, :], top_diag, start=True, stop=True))
        wait(dve, t)
        v_done.mark(dve.memset(w0_i[:, 0:LAG], 0))
        v_done.mark(dve.tensor_copy(w0_i[:, LAG:LAG + NG], x_ps[0:1, 0:NG]))
        wait(dve, v_done.now())
        v_done.mark(dve.tensor_copy(adj_at[:, :], x_ps[:, 0:NG]))
        top = tA[:, 512:512 + NG]
        v_done.mark(dve.tensor_copy(top, x_ps[:, 128:128 + NG]))
        wait(dve, v_done.now())
        t = v_done.mark(dve.memset(adj_at[:, 0:1], 0.0))
        wait(dve, t)
        v_done.mark(dve.tensor_copy(adj_at_i[:, :], adj_at[0:1, :]))
        a_, flags = adj_at[0:1, :], tA[0:1, 2048:2048 + 4 * NG]
        step, span, over, end = (flags[:, k * NG:(k + 1) * NG] for k in range(4))
        v_done.mark(dve.memset(flags, 0.0))
        wait(dve, v_done.now())
        v_done.mark(dve.tensor_tensor(step[:, 1:NG], a_[:, 1:NG], a_[:, 0:NG - 1], ALU.subtract))
        v_done.mark(dve.tensor_tensor(span, top[0:1, :], a_, ALU.subtract))
        v_done.mark(dve.tensor_tensor(over[:, 1:NG], top[0:1, 0:NG - 1], a_[:, 1:NG], ALU.subtract))
        v_done.mark(dve.tensor_scalar(end[:, 0:1], a_[:, NG - 1:NG], float(NP - D - ADJ_WIN), None, ALU.is_lt))
        wait(dve, v_done.now())
        t = v_done.mark(dve.tensor_scalar(carry_f, step, 0.0, float(ADJ_WIN - 1), ALU.max, ALU.min))
        wait(dve, t)
        v_done.mark(dve.tensor_scalar(carry_i[:, :], carry_f, float(N_TILES), None, ALU.mult))
        v_done.mark(dve.tensor_scalar(step, step, float(ADJ_WIN), None, ALU.is_ge))
        v_done.mark(dve.tensor_scalar(span, span, float(ADJ_WIN), None, ALU.is_ge))
        v_done.mark(dve.tensor_scalar(over, over, 0.0, None, ALU.is_gt))
        wait(dve, v_done.now())
        v_done.mark(dve.tensor_reduce(small[0:1, 12:13], flags, AX.X, ALU.add))
        lane_i, tile_i = tA[:, 2560:2560 + NG * GC].bitcast(I32), src_i
        v_done.mark(dve.tensor_scalar(lane_i, src_i, D - 1, None, ALU.bitwise_and))
        wait(dve, v_done.now())
        v_done.mark(dve.tensor_copy(lane[:, :], lane_i))
        v_done.mark(dve.tensor_scalar(tile_i, src_i, D.bit_length() - 1, None, ALU.arith_shift_right))
        k3 = key[:, :].rearrange("p (g k) -> p g k", k=GC)
        v_done.mark(dve.tensor_tensor(k3, dst_rel[:, :].rearrange("p (g k) -> p g k", k=GC),
                                      adj_at[:, :].unsqueeze(2).to_broadcast([D, NG, GC]), ALU.subtract))
        wait(dve, v_done.now())
        v_done.mark(dve.tensor_copy(lane_f, tile_i))
        wait(dve, v_done.now())
        v_done.mark(dve.scalar_tensor_tensor(out=key[:, :], in0=key[:, :], scalar=float(N_TILES), in1=lane_f,
                                             op0=ALU.mult, op1=ALU.add))
        v_done.mark(dve.tensor_copy(key_no[:, :], node_no[:, 0:ADJ_WIN * N_TILES]))
        v_done.mark(dve.tensor_copy(ident_bf[:, :], ident[:, :]))
        v_done.mark(dve.memset(adj_ring[:, 1, :], 0.0))
        zeros = as_bf16(acc[:, 1, 0:D * N_TILES // 2], D * N_TILES)
        t = v_done.mark(dve.memset(zeros, 0.0))
        wait(act, t)
        adj_st.mark(act.dma_start(adj[:, NP - D:NP, :].rearrange("p d t -> p (d t)"), zeros))
        wait(dve, part_no)
        v_done.mark(dve.tensor_scalar(small[0:WIN, 9:10], far, 4.0 * NP, small[0:WIN, 10:11], ALU.mult, ALU.add))
        wait(dve, v_done.now())
        v_done.mark(dve.tensor_scalar(win_node[:, :], x_ps[0:WIN, 0:NG], small[0:WIN, 9:10], None, ALU.add))
        d3 = dst_rel[:, :].rearrange("p (g k) -> p g k", k=GC)
        windows = v_done.mark(dve.tensor_tensor(d3, d3, x_ps[:, 0:NG].unsqueeze(2).to_broadcast([D, NG, GC]),
                                                ALU.subtract))
        wait(dve, windows)
        wait(pe, windows)
        wide_v = dve.value_load(any_wide[0:1, 0:1], min_val=0, max_val=NG)
        wide_p = pe.value_load(any_wide[0:1, 0:1], min_val=0, max_val=NG)

        def load_idx(g, j, srcs, done):
            hold(sp, (done.sem, done.n + g - (UNROLL - 1)))
            for k, a in enumerate(srcs):
                sp.dma_start(idx_ring[:, j, k, :], a[bass.ds(g, 1), :, :].rearrange("a p k -> (a p) k")
                             ).then_inc(idx_in[j].sem, 16)

        def gather(i, j, tables, free, done=None):
            hold(pool, (idx_in[j].sem, idx_in[j].n + 16 * len(tables) * (i + 1)), *free)
            for k, t in enumerate(tables):
                gather_rows(j, k, t, done or rows_in)

        def gather_rows(j, k, table_at_width, done):
            table, at, width = table_at_width
            for c in range(GC):
                pool.indirect_dma_start(m_ring[j][:, c, at:at + width], None, table[:, :],
                                        bass.IndirectOffsetOnAxis(ap=idx_ring[:, j, k, c:c + 1], axis=0)
                                        ).then_inc(done[j].sem, 16)

        def rows_ready(i, j, rows=None):
            q = (rows or rows_in)[j]
            return (q.sem, q.n + 16 * GC * (i + 1))

        def e_ready(i, j, loads=1):
            q = e_in[j % E_SLOTS]
            return (q.sem, q.n + 16 * loads * (i * (UNROLL // E_SLOTS) + j // E_SLOTS + 1))

        def load_e(g, j):
            hold(sp, (ve_mm.sem, ve_mm.n + g - (E_SLOTS - 1)))
            sp.dma_start(e_ring[:, j % E_SLOTS, :], e_t[:, bass.ds(g * GE, GE)]).then_inc(e_in[j % E_SLOTS].sem, 16)

        def window_start(g):
            return dve.value_load(w0_i[0:1, bass.ds(g + LAG, 1)], min_val=0, max_val=N_NODES - 1)

        def one_hot(g, j):
            wait(dve, (sc_mm.sem, sc_mm.n + g - (OH_SLOTS - 1)))
            dve.tensor_tensor(oh_ring[:, j % OH_SLOTS, :, :], node_no[:, 0:WIN].unsqueeze(1).to_broadcast([D, GC, WIN]),
                              dst_rel[:, bass.ds(g * GC, GC)].unsqueeze(2).to_broadcast([D, GC, WIN]),
                              ALU.is_equal).then_inc(oh.sem, 1)

        def wide_mm(g, channels):
            with pe.If(wide_p > 0):
                with pe.Fori(1, N_WIN) as k:
                    at = g * (N_WIN - 1) + k
                    wait(pe, (oh_x.sem, oh_x.n + at))
                    for h, (lhs, m) in enumerate(channels):
                        for c in range(GC):
                            mm = pe.matmul(x_ps[0:m, h * WIN:(h + 1) * WIN], lhs(c), oh_wide[:, c, :],
                                           start=(c == 0), stop=(c == GC - 1))
                    mm.then_inc(mm_x.sem, 1)

        def wide_add(g, sums):
            with dve.If(wide_v > 0):
                with dve.Fori(1, N_WIN) as k:
                    at = g * (N_WIN - 1) + k
                    dve.tensor_tensor(oh_wide[:, :, :],
                                      node_no[:, bass.ds(k * WIN, WIN)].unsqueeze(1).to_broadcast([D, GC, WIN]),
                                      dst_rel[:, bass.ds(g * GC, GC)].unsqueeze(2).to_broadcast([D, GC, WIN]),
                                      ALU.is_equal).then_inc(oh_x.sem, 1)
                    wait(dve, (mm_x.sem, mm_x.n + at))
                    for h, (array, m) in enumerate(sums):
                        a = array[0:m, bass.ds(k * WIN, WIN)]
                        add = dve.tensor_tensor(a, a, x_ps[0:m, h * WIN:(h + 1) * WIN], ALU.add)
                    add.then_inc(add_x.sem, 1)
                    wait(dve, (add_x.sem, add_x.n + at))

        def segment_mm(g, j, ready, channels):
            wait(pe, *ready)
            wide_mm(g, channels)
            wait(pe, (oh.sem, oh.n + g + 1))
            wait(pe, (sc_add.sem, sc_add.n + g - 1))
            for h, (lhs, m) in enumerate(channels):
                for c in range(GC):
                    mm = pe.matmul(acc_ps[0:m, j % 2, h * WIN:(h + 1) * WIN], lhs(c), oh_ring[:, j % OH_SLOTS, c, :],
                                   start=(c == 0), stop=(c == GC - 1))
            mm.then_inc(sc_mm.sem, 1)

        def segment_add(g, w0, product, ps, sums):
            wait(dve, (product.sem, product.n + g + 1))
            wait(dve, (sc_add.sem, sc_add.n + g))
            for h, (array, m) in enumerate(sums):
                a = array[0:m, bass.ds(w0, WIN)]
                add = dve.tensor_tensor(a, a, ps[0:m, h * WIN:(h + 1) * WIN], ALU.add)
            add.then_inc(sc_add.sem, 1)

        def window_ps(slot):
            return banks[:, 2 * slot + 1, 0:2 * WIN]

        def start_windows():
            v_done.mark(dve.memset(acc_ps[0:WIN, 1, 0:2 * D], 0.0))
            t = v_done.mark(dve.memset(window_ps(0), 0.0))
            wait(dve, t)
            wait(act, t)
            wait(pe, t)

        def window_mm(g, j, halves):
            wait(pe, (oh.sem, oh.n + g + 1))
            wait(pe, (win_out.sem, win_out.n + g))
            for c in range(GC):
                mm = pe.matmul(acc_ps[0:WIN, j % 2, 0:halves * D], oh_ring[:, j % OH_SLOTS, c, :],
                               m_ring[j][:, c, 0:halves * D], start=(c == 0), stop=(c == GC - 1))
            mm.then_inc(sc_mm.sem, 1)

        def window_out(b, slot, halves):
            wait(act, (sc_mm.sem, sc_mm.n + b))
            wait(act, (win_t.sem, win_t.n + b - 1))
            act.copy(win_ring[:, slot, 0:halves * D], acc_ps[0:WIN, slot, 0:halves * D]).then_inc(win_out.sem, 1)

        def transpose_window(b, slot, halves):
            wait(pe, (win_out.sem, win_out.n + b + 1))
            hold(pe, (sc_add.sem, sc_add.n + b))
            for h in range(halves):
                mm = pe.transpose(window_ps(slot)[:, h * WIN:(h + 1) * WIN],
                                  win_ring[:, slot, h * D:(h + 1) * D], ident[0:WIN, 0:WIN])
            mm.then_inc(win_t.sem, 1)

        def add_window(a, w0, slot, halves):
            wait(dve, (win_t.sem, win_t.n + a))
            wait(dve, (sc_add.sem, sc_add.n + a))
            to = acc[:, 0:halves, bass.ds(w0, WIN)]
            dve.tensor_tensor(to, to, window_ps(slot)[:, 0:halves * WIN].rearrange("p (h n) -> p h n", h=halves), ALU.add
                              ).then_inc(sc_add.sem, 1)

        def finish_windows(halves):
            window_out(NG, (NG + 1) % 2, halves)
            transpose_window(NG, (NG + 1) % 2, halves)
            for a in range(NG, NG + LAG):
                add_window(a, window_start(a - LAG), a % 2, halves)
            win_out.n += NG + 1
            win_t.n += NG + 1
            sc_add.n += LAG
            segments_counted()

        def segments_counted():
            for c in (oh, sc_mm, sc_add):
                c.n += NG
            for c in (oh_x, mm_x, add_x):
                c.n += NG * (N_WIN - 1)

        def rings_counted(idx=0, e=0, rows=0, pre_o=0, pre_i=0):
            for qs, k in ((idx_in, idx), (e_in, e), (rows_in, GC * rows), (pre_out, pre_o), (pre_in, pre_i)):
                for q in qs:
                    q.n += 16 * k * NG // len(qs)

        def clear_acc(halves):
            return [v_done.mark(dve.memset(acc[:, h, :], 0.0)) for h in range(halves)]

        def adj_one_hots(g, j):
            wait(dve, (adj_mm.sem, adj_mm.n + g - 1))
            dve.tensor_tensor(lane_ring[:, j % 2, :, :], node_no[:, 0:D].unsqueeze(1).to_broadcast([D, GC, D]),
                              lane[:, bass.ds(g * GC, GC)].unsqueeze(2).to_broadcast([D, GC, D]), ALU.is_equal)
            for c in range(GC):
                last = dve.tensor_scalar(key_ring[j % 2][:, c, :], key_no[:, :], key[:, bass.ds(g * GC + c, 1)], None,
                                         ALU.is_equal)
            last.then_inc(key_oh.sem, 1)

        def adj_product(g, j):
            at = pe.value_load(carry_i[0:1, bass.ds(g, 1)], min_val=0, max_val=(ADJ_WIN - 1) * N_TILES)
            wait(pe, (key_oh.sem, key_oh.n + g + 1))
            hold(pe, (adj_cp.sem, adj_cp.n + g))
            half = ADJ_WIN // 2 * N_TILES
            for h in range(2):
                for c in range(GC):
                    mm = pe.matmul(banks[:, 2 * (j % 2) + h, 0:half], lane_ring[:, j % 2, c, :],
                                   key_ring[j % 2][:, c, h * half:(h + 1) * half],
                                   start=(c == 0), stop=(h == 1 and c == GC - 1), skip_group_check=True)
            pe.matmul(banks[:, 2 * (j % 2), 0:N_TILES], ident_bf[:, :], adj_ring[:, (j + 1) % 2, bass.ds(at, N_TILES)],
                      start=False, stop=True, skip_group_check=True).then_inc(adj_mm.sem, 1)

        def adj_store(g, j):
            wait(act, (adj_mm.sem, adj_mm.n + g + 1))
            half = ADJ_WIN // 2 * N_TILES
            act.copy(adj_ring[:, j % 2, :].rearrange("p (h k) -> p h k", h=2),
                     banks[:, 2 * (j % 2):2 * (j % 2) + 2, 0:half]).then_inc(adj_cp.sem, 1)
            first = act.value_load(adj_at_i[0:1, bass.ds(g, 1)], min_val=0, max_val=N_NODES - 1)
            hold(act, (adj_st.sem, adj_st.n + 16 * g))
            hold(act, (adj_cp.sem, adj_cp.n + g + 1))
            act.dma_start(adj[:, bass.ds(first, ADJ_WIN), :].rearrange("p d t -> p (d t)"), adj_ring[:, j % 2, :]
                          ).then_inc(adj_st.sem, 16)

        def sum_neighbours(table, ready, rows, first=False):
            wait(dve, cleared.mark(dve.memset(acc[:, 0, :], 0.0)))
            wait(pool, *ready)
            wait(sp, sc_mm.now(), st_mm.now())
            sums = [(acc[:, 0, :], D)] + ([(deg, 1)] if first else [])
            with nc.Fori(0, NG // UNROLL) as i:
                for j in range(UNROLL):
                    g = i * UNROLL + j
                    load_idx(g, j, [src_g], sc_mm)
                    gather(i, j, [(table, 0, D)], [(sc_mm.sem, sc_mm.n + g - (UNROLL - 1))], rows)
                    if first:
                        adj_one_hots(g, j)
                        adj_product(g, j)
                        adj_store(g, j)
                    wide_add(g, sums)
                    one_hot(g, j)
                    if j:
                        segment_add(g - 1, window_start(g - 1), sc_mm, acc_ps[:, (j - 1) % 2, :], sums)
                    chans = [(lambda c, j=j: m_ring[j][:, c, 0:D], D)] + (
                        [(lambda c: ones[:, 0:1], 1)] if first else [])
                    segment_mm(g, j, [rows_ready(i, j, rows)], chans)
                segment_add(g, window_start(g), sc_mm, acc_ps[:, j % 2, :], sums)
            rings_counted(idx=1)
            for q in rows:
                q.n += 16 * GC * NG // UNROLL
            segments_counted()
            if first:
                for c in (key_oh, adj_mm, adj_cp):
                    c.n += NG
                adj_st.n += 16 * NG
            return sc_add.now()

        def bf16_parts(src3, ready):
            rest = acc[:, 0, :].rearrange("p (t f) -> p t f", f=D)
            wait(act, *ready)
            wait(dve, *ready)
            halves = [slice(0, N_TILES // 2), slice(N_TILES // 2, N_TILES)]
            t = [a_done.mark(act.copy(parts[0][:, h, :], src3[:, h, :])) for h in halves]
            for k, source in ((1, src3), (2, rest)):
                for n, h in enumerate(halves):
                    wait(dve, t[n])
                    t[n] = v_done.mark(dve.tensor_tensor(rest[:, h, :], source[:, h, :], parts[k - 1][:, h, :],
                                                         ALU.subtract))
                    wait(act, t[n])
                    t[n] = a_done.mark(act.copy(parts[k][:, h, :], rest[:, h, :]))
            return t[1]

        def adjacency_product(ready, slot_free):
            wait(sp, *slot_free)
            wait(pe, *ready)
            wait(act, *ready)
            blocks_ = NP // ADJ_BLOCK
            with nc.Fori(0, blocks_ // 2) as i:
                for k in range(2):
                    b = i * 2 + k
                    hold(sp, (block_mm.sem, block_mm.n + b - 1))
                    if k:
                        wait(sp, *ready)
                    sp.dma_start(adj_in[k].rearrange("p d t -> p (d t)"),
                                 adj[:, bass.ds(b * ADJ_BLOCK, ADJ_BLOCK), :].rearrange("p d t -> p (d t)")
                                 ).then_inc(block_in[k].sem, 16)
                    wait(pe, (block_in[k].sem, block_in[k].n + 16 * (i + 1)))
                    wait(pe, (block_out.sem, block_out.n + b - 1))
                    for n, (t, part) in enumerate((t, part) for t in range(N_TILES) for part in parts):
                        mm = pe.matmul(banks[:, k, 0:ADJ_BLOCK], part[:, t, :], adj_in[k][:, :, t],
                                       start=(n == 0), stop=(n == 3 * N_TILES - 1))
                    mm.then_inc(block_mm.sem, 1)
                    hold(act, (block_mm.sem, block_mm.n + b + 1))
                    act.copy(acc[:, 0, bass.ds(b * ADJ_BLOCK, ADJ_BLOCK)], banks[:, k, 0:ADJ_BLOCK]
                             ).then_inc(block_out.sem, 1)
            for q in (block_mm, block_out):
                q.n += blocks_
            for q in block_in:
                q.n += 16 * blocks_ // 2

        def sum_neighbours_again(src3, ready):
            slot_free = [sc_mm.now()]
            t = bf16_parts(src3, ready)
            at_ease = [t, v_done.now()] + [m for m in bank_free if m]
            with nc.If(gather_again > 0):
                wait(dve, *at_ease)
                wait(sp, *at_ease)
                stored = table_again.mark(sp.dma_start(tab0.rearrange("(t p) f -> p t f", p=D), src3))
                sum_neighbours(tab0, [*at_ease, stored], rows_again)
                wait(dve, sc_add.now())
            with nc.Else():
                adjacency_product(at_ease, slot_free)
                wait(dve, block_out.now())
                for n, (q, k) in enumerate([(sc_mm, NG), (sc_add, NG), (oh, NG)]
                                           + [(q, 16 * NG // UNROLL) for q in idx_in]):
                    dve.memset(small[:, 32 + n:33 + n], 0.0).then_inc(q.sem, k)
            t = v_done.mark(dve.memset(small[:, 14:15], 0.0))
            for k in range(4):
                bank_free[k] = t
            return t

        bank_free = [None] * 4
        turn = [0]

        def bank():
            b = turn[0] % 4
            turn[0] += 1
            return b

        def blocks():
            return [(a, min(a + 512, NP)) for a in range(0, NP, 512)]

        def product_T(terms, ready, evacuate):
            wait(pe, *ready)
            for a, b in blocks():
                k = bank()
                if bank_free[k]:
                    wait(pe, bank_free[k])
                for n, (lhs, rhs) in enumerate(terms):
                    mm = pe.matmul(banks[:, k, 0:b - a], lhs, rhs[:, a:b], start=(n == 0), stop=(n == len(terms) - 1))
                done = p_done.mark(mm)
                bank_free[k] = evacuate(banks[:, k, 0:b - a], a, b, done)
                last = bank_free[k]
            return last

        def to_act(out_, func, bias, scale=1.0):
            def evacuate(ps, a, b, done):
                wait(act, done)
                return a_done.mark(act.activation(out_[:, a:b], ps, func, bias=bias, scale=scale))
            return evacuate

        def turn_tiles(src_tile, out_block, ready):
            wait(pe, *ready)
            marks = []
            for t0 in range(0, N_TILES, 4):
                n = min(4, N_TILES - t0)
                k = bank()
                if bank_free[k]:
                    wait(pe, bank_free[k])
                for q in range(n):
                    done = p_done.mark(pe.transpose(banks[:, k, q * D:(q + 1) * D], src_tile(t0 + q), ident[:, :]))
                eng, cnt = (dve, v_done) if (t0 // 4) % 2 else (act, a_done)
                wait(eng, done)
                o, s = out_block(t0, n), banks[:, k, 0:n * D]
                bank_free[k] = cnt.mark(eng.tensor_copy(o, s) if eng is dve else eng.copy(o, s))
                marks.append(bank_free[k])
            return marks[-2:]

        def N_to_T(src3, out_, ready):
            marks = turn_tiles(lambda t: src3[:, t, :], lambda t0, n: out_[:, t0 * D:(t0 + n) * D], ready)
            wait(dve, *marks)
            return [v_done.mark(dve.memset(out_[:, N_NODES:NP], 0.0))]

        def node_table(src, rhs, width, ready, table, at=0, bias=None):
            wait(pe, *ready)
            per = 512 // width
            marks, stored = [], 0
            for t0 in range(0, N_TILES, per):
                n = min(per, N_TILES - t0)
                k = bank()
                if bank_free[k]:
                    wait(pe, bank_free[k])
                for q in range(n):
                    mm = pe.matmul(banks[:, k, q * width:(q + 1) * width], src[:, (t0 + q) * D:(t0 + q + 1) * D], rhs,
                                   start=True, stop=True)
                done = p_done.mark(mm)
                eng, cnt = (dve, v_done) if (t0 // per) % 2 or bias is not None else (act, a_done)
                wait(eng, done)
                o = tN[:, t0:t0 + n, at:at + width]
                s = banks[:, k, 0:n * width].rearrange("p (t f) -> p t f", f=width)
                if bias is not None:
                    b = bias.unsqueeze(1).to_broadcast([D, n, width])
                    bank_free[k] = cnt.mark(dve.tensor_tensor(o, s, b, ALU.add))
                else:
                    bank_free[k] = cnt.mark(eng.tensor_copy(o, s) if eng is dve else eng.copy(o, s))
                marks.append(bank_free[k])
                if t0 + n - stored >= 8 or t0 + n == N_TILES:
                    wait(sp, *marks[-2:])
                    t = table_w.mark(sp.dma_start(
                        table[stored * D:(t0 + n) * D, :].rearrange("(t p) f -> p t f", p=D),
                        tN[:, stored:t0 + n, at:at + width]))
                    stored = t0 + n
            return t

        def norm_N(v3, ready, tmp3):
            mean, var, std, inv = (vec[:, k * N_TILES:(k + 1) * N_TILES] for k in range(4))
            wait(dve, *ready)
            t = v_done.mark(dve.tensor_reduce(mean, v3, AX.X, ALU.add))
            wait(dve, t)
            t = v_done.mark(dve.tensor_scalar(mean, mean, 1.0 / D, None, ALU.mult))
            wait(dve, t)
            halves, squared = [slice(0, N_TILES // 2), slice(N_TILES // 2, N_TILES)], []
            for h in halves:
                n = h.stop - h.start
                t = v_done.mark(dve.tensor_tensor(v3[:, h, :], v3[:, h, :], mean[:, h].unsqueeze(2)
                                                  .to_broadcast([D, n, D]), ALU.subtract))
                wait(act, t)
                squared.append(a_done.mark(act.activation(tmp3[:, h, :], v3[:, h, :], ACT.Square)))
            for h, t in zip(halves, squared):
                wait(dve, t)
                t = v_done.mark(dve.tensor_reduce(var[:, h], tmp3[:, h, :], AX.X, ALU.add))
            wait(act, t)
            t = a_done.mark(act.activation(std, var, ACT.Sqrt, bias=eps_c[:, :], scale=1.0 / D))
            wait(dve, t)
            t = v_done.mark(dve.reciprocal(inv, std))
            wait(dve, t)
            return v_done.mark(dve.tensor_tensor(v3, v3, inv.unsqueeze(2).to_broadcast([D, N_TILES, D]), ALU.mult))

        def add_and_norm(yT, ready):
            y3 = tN[:, :, 0:D]
            marks = T_to_N_wide(yT, ready)
            wait(dve, *marks)
            t = v_done.mark(dve.tensor_tensor(xN[:, :, :], xN[:, :, :], y3, ALU.add))
            return norm_N(xN[:, :, :], [t], y3)

        def T_to_N_wide(src, ready):
            wait(pe, *ready)
            marks = []
            for t0 in range(0, N_TILES, 4):
                n = min(4, N_TILES - t0)
                k = bank()
                if bank_free[k]:
                    wait(pe, bank_free[k])
                for q in range(n):
                    done = p_done.mark(pe.transpose(banks[:, k, q * D:(q + 1) * D],
                                                    src[:, (t0 + q) * D:(t0 + q + 1) * D], ident[:, :]))
                eng, cnt = (dve, v_done) if (t0 // 4) % 2 else (act, a_done)
                wait(eng, done)
                o, s = tN[:, t0:t0 + n, 0:D], banks[:, k, 0:n * D].rearrange("p (t f) -> p t f", f=D)
                bank_free[k] = cnt.mark(eng.tensor_copy(o, s) if eng is dve else eng.copy(o, s))
                marks.append(bank_free[k])
            return marks[-2:]

        one = v_done.mark(dve.tensor_scalar(one_eps[:, :], one_eps[:, :], 1.0, None, ALU.add))

        def gin(layer, inT, wa, ba, g_, bt, wb, bb, func, summed):
            a0 = acc[:, 0, :]
            hid = acc[:, 1, :]
            c = chan
            wait(dve, summed, one)
            t = v_done.mark(dve.scalar_tensor_tensor(out=a0, in0=inT[:, :], scalar=one_eps[:, layer:layer + 1], in1=a0,
                                                     op0=ALU.mult, op1=ALU.add))
            t = product_T([(W(wa), a0)], [t], to_act(hid, ACT.Identity, col(ba)))
            wait(dve, t)
            t = v_done.mark(dve.tensor_reduce(c[:, 0:1], hid[:, 0:N_NODES], AX.X, ALU.add))
            wait(dve, t)
            t = v_done.mark(dve.tensor_scalar(c[:, 1:2], c[:, 0:1], -1.0 / N_NODES, None, ALU.mult))
            wait(act, t)
            t = a_done.mark(act.activation(a0[:, 0:N_NODES], hid[:, 0:N_NODES], ACT.Square, bias=c[:, 1:2],
                                           accum_out=c[:, 2:3]))
            wait(act, t)
            t = a_done.mark(act.activation(c[:, 3:4], c[:, 2:3], ACT.Sqrt, bias=eps_c[:, :], scale=1.0 / N_NODES))
            wait(dve, t)
            t = v_done.mark(dve.reciprocal(c[:, 4:5], c[:, 3:4]))
            wait(dve, t)
            t = v_done.mark(dve.tensor_tensor(c[:, 5:6], c[:, 4:5], col(g_), ALU.mult))
            wait(dve, t)
            t = v_done.mark(dve.scalar_tensor_tensor(out=c[:, 6:7], in0=c[:, 1:2], scalar=c[:, 5:6], in1=col(bt),
                                                     op0=ALU.mult, op1=ALU.add))
            wait(act, t)
            t = a_done.mark(act.activation(a0, hid, ACT.Relu, bias=c[:, 6:7], scale=c[:, 5:6]))
            return product_T([(W(wb), a0)], [t], to_act(tA, func, col(bb)))

        s = sum_neighbours(x_n, [], rows_in, first=True)
        wait(dve, s)
        v_done.mark(dve.tensor_reduce(small[0:1, 13:14], deg[:, :], AX.X, ALU.max))
        wait(dve, v_done.now())
        t = v_done.mark(dve.tensor_scalar(small[0:1, 13:14], small[0:1, 13:14], float(MAX_COUNT), small[0:1, 12:13],
                                          ALU.is_gt, ALU.add))
        wait(dve, t)
        t = v_done.mark(dve.tensor_copy(irregular[:, :], small[0:1, 13:14]))
        for eng in (pe, dve, act, pool, sp):
            wait(eng, t)
            eng.nop(nofuse=True)
        gather_again = nc.values_load(irregular[0:1, 0:1], min_val=0, max_val=4 * NG + 1)
        for k in range(4):
            bank_free[k] = adj_cp.now()
        wait(sp, adj_st.now())
        t = gin(0, xT, "w1a", "b1a", "g1", "bt1", "w1b", "b1b", ACT.Relu, s)
        m = T_to_N_wide(tA, [t])
        s = sum_neighbours_again(tN[:, :, 0:D], m)
        t = gin(1, tA, "w2a", "b2a", "g2", "bt2", "w2b", "b2b", ACT.Identity, s)
        xn_ready = add_and_norm(tA, [t])
        xt_ready = N_to_T(xN, xT, [xn_ready])

        def block1(xn_ready, xt_ready):
            node_table(xT, W("msg_xs"), D, xt_ready, tabs)
            t = node_table(xT, W("msg_xd"), D, [], tabd, at=D, bias=row("msg_b1"))
            wait(dve, *clear_acc(1))
            wait(pool, t)
            start_windows()
            wait(pool, windows)
            wide_g = pool.value_load(any_wide[0:1, 0:1], min_val=0, max_val=NG)
            wait(sp, windows, t, sc_mm.now(), st_mm.now())

            def load_window(g, j):
                slot = j % E_SLOTS
                hold(sp, (ohT.sem, ohT.n + g - (E_SLOTS - 1)))
                sp.dma_start(dst_ring[:, slot, :], dst_row[bass.ds(g, 1), :].partition_broadcast(WIN)
                             .rearrange("p a f -> p (a f)")).then_inc(e_in[slot].sem, 16)
                w0 = sp.value_load(w0_i[0:1, bass.ds(g + LAG, 1)], min_val=0, max_val=N_NODES - 1)
                sp.dma_start(tabd_ring[:, slot, :], tabd[bass.ds(w0, WIN), :]).then_inc(e_in[slot].sem, 16)

            def one_hot_T(i, j):
                g = i * UNROLL + j
                wait(dve, e_ready(i, j, loads=3))
                wait(dve, (ve_mm.sem, ve_mm.n + g - 1))
                dve.tensor_tensor(ohT_ring[:, j % 2, :], dst_ring[:, j % E_SLOTS, :],
                                  win_node[:, bass.ds(g, 1)].to_broadcast([WIN, GE]),
                                  ALU.is_equal).then_inc(ohT.sem, 1)

            def edge_product(i, j):
                g = i * UNROLL + j
                wait(pe, e_ready(i, j, loads=3))
                wait(pe, (ohT.sem, ohT.n + g + 1))
                wait(pe, (pre.sem, pre.n + g - 1))
                for c in range(GC):
                    part, edges = banks[:, 2 * (j % 2), c * D:(c + 1) * D], slice(c * D, (c + 1) * D)
                    pe.matmul(part, e_ring[:, j % E_SLOTS, edges], W("msg_e"), start=True, stop=False)
                    mm = pe.matmul(part, ohT_ring[:, j % 2, edges], tabd_ring[:, j % E_SLOTS, :],
                                   start=False, stop=True)
                mm.then_inc(ve_mm.sem, 1)

            sums = [(acc[:, 0, :], D)]
            with nc.Fori(0, NG // UNROLL) as i:
                one_hot_T(i, 0)
                edge_product(i, 0)
                for j in range(UNROLL):
                    g = i * UNROLL + j
                    free = [(sc_mm.sem, sc_mm.n + g - (UNROLL - 1))]
                    load_idx(g, j, [src_g, dst_g], sc_mm)
                    load_e(g, j)
                    load_window(g, j)
                    hold(pool, (idx_in[j].sem, idx_in[j].n + 32 * (i + 1)), *free)
                    with pool.If(wide_g > 0):
                        gather_rows(j, 1, (tabd, D, D), rows_x)
                    gather_rows(j, 0, (tabs, 0, D), rows_in)
                    hold(dve, rows_ready(i, j))
                    a, b = m_ring[j][:, :, 0:D], m_ring[j][:, :, D:2 * D]
                    with dve.If(wide_v > 0):
                        wait(dve, (rows_x[j].sem, rows_x[j].n + 16 * GC * (i + 1)))
                        dve.tensor_tensor(a, a, b, ALU.add).then_inc(pre_x.sem, 1)
                        hold(dve, (pre_x.sem, pre_x.n + g + 1))
                    wait(dve, (ve_mm.sem, ve_mm.n + g + 1))
                    dve.tensor_tensor(a, a, banks[:, 2 * (j % 2), :].rearrange("p (c f) -> p c f", f=D),
                                      ALU.add).then_inc(pre.sem, 1)
                    if j + 1 < UNROLL:
                        one_hot_T(i, j + 1)
                    w0 = window_start(g - LAG)
                    wide_add(g, sums)
                    one_hot(g, j)
                    add_window(g, w0, j % 2, 1)
                    wait(act, (pre.sem, pre.n + g + 1))
                    act.activation(a, a, ACT.Silu).then_inc(sq.sem, 1)
                    if j + 1 < UNROLL:
                        edge_product(i, j + 1)
                    wait(pe, (sq.sem, sq.n + g + 1))
                    wide_mm(g, [(lambda c, j=j: m_ring[j][:, c, 0:D], D)])
                    window_mm(g, j, 1)
                    transpose_window(g, (j + 1) % 2, 1)
                    window_out(g, (j + 1) % 2, 1)
            finish_windows(1)
            rings_counted(idx=2, e=3, rows=1)
            for c in (ve_mm, pre, sq, ohT):
                c.n += NG
            for k in range(4):
                bank_free[k] = sc_add.now() if k % 2 else pre.now()

            a0, a1 = acc[:, 0, :], acc[:, 1, :]
            t = product_T([(W("msg_2"), a0), (row("msg_b2")[0:1, :], deg)], [sc_add.now()], to_act(a1, ACT.Identity, 0.0))
            t = product_T([(W("upd_x"), xT), (W("upd_a"), a1)], [t, *xt_ready], to_act(a0, ACT.Silu, col("upd_b1")))
            t = product_T([(W("upd_2"), a0)], [t], to_act(tA, ACT.Identity, col("upd_b2")))
            y3 = tN[:, :, 0:D]
            m = T_to_N_wide(tA, [t])
            wait(dve, *m)
            t = v_done.mark(dve.tensor_tensor(y3, y3, xN[:, :, :], ALU.add))
            t = norm_N(y3, [t], tN[:, :, D:2 * D])
            wait(dve, t)
            t = v_done.mark(dve.tensor_tensor(y3, y3, row("ln_g").unsqueeze(1).to_broadcast([D, N_TILES, D]), ALU.mult))
            wait(dve, t)
            t = v_done.mark(dve.tensor_tensor(y3, y3, row("ln_b").unsqueeze(1).to_broadcast([D, N_TILES, D]), ALU.add))
            wait(dve, t)
            t = v_done.mark(dve.tensor_tensor(xN[:, :, :], xN[:, :, :], y3, ALU.add))
            xn = norm_N(xN[:, :, :], [t], y3)
            return xn, N_to_T(xN, xT, [xn])

        def block2(xn_ready, xt_ready):
            hT, h_ready = xT, list(xt_ready)
            for l in range(N_LAYERS2):
                c = chan
                SG, AB, B1, MEAN, EX2, VAR, S, SH, LOW = (c[:, 2 * k:2 * k + 2] for k in range(9))
                gam, bet, b1 = (col_all[:, COLS.index(f"{k}{l}0"):COLS.index(f"{k}{l}0") + 2] for k in ("g", "bt", "b"))
                t = v_done.mark(dve.tensor_scalar(SG, gam, 0.0, 2.0, ALU.is_ge, ALU.mult))
                wait(dve, t)
                t = v_done.mark(dve.tensor_scalar(SG, SG, -1.0, None, ALU.add))
                wait(dve, t)
                v_done.mark(dve.tensor_tensor(B1, SG, b1, ALU.mult))
                t = v_done.mark(dve.tensor_tensor(AB, SG, gam, ALU.mult))
                wait(dve, t)
                t = v_done.mark(dve.tensor_scalar(AB, AB, TINY, None, ALU.max))

                def spread(cols2, dst, t):
                    for h in range(2):
                        wait(dve, t)
                        t = v_done.mark(dve.tensor_scalar(diag[:, :], ident[:, :], cols2[:, h:h + 1], None, ALU.mult))
                        wait(pe, t)
                        t = p_done.mark(pe.matmul(x_ps[:, 0:D], ones[:, :], diag[:, :], start=True, stop=True))
                        wait(dve, t)
                        t = v_done.mark(dve.tensor_copy(dst[:, h * D:(h + 1) * D], x_ps[:, 0:D]))
                    return t

                t = spread(SG, sgn, t)
                wait(dve, t)
                v_done.mark(dve.tensor_tensor(W(f"eh{l}"), W(f"eh{l}"), sgn[:, :], ALU.mult))
                t = v_done.mark(dve.tensor_tensor(W(f"ee{l}"), W(f"ee{l}"), sgn[:, :], ALU.mult))
                t = node_table(hT, W(f"eh{l}"), 2 * D, [t] + h_ready, tab2)
                wait(pool, t)
                wait(sp, sc_mm.now(), st_mm.now())
                zero = small[:, 8:9]
                sq_acc = acc[:, 0, 0:GC * 2 * D]
                clear_acc(2)
                t = v_done.mark(dve.memset(zero, 0.0))
                wait(pe, t)
                wait(dve, t)
                pe.matmul(st_ps[0:1, :], zero, node_no[:, 0:512], start=True, stop=False, skip_group_check=True)

                def relu_e(i, j):
                    if l:
                        hold(act, e_ready(i, j))
                        e = e_ring[:, j % E_SLOTS, :]
                        act.activation(e, e, ACT.Relu).then_inc(e_relu.sem, 1)

                def edge_product(i, j):
                    g = i * UNROLL + j
                    wait(pe, (e_relu.sem, e_relu.n + g + 1) if l else e_ready(i, j))
                    wait(pe, (pre.sem, pre.n + g - 1))
                    for c_ in range(GC):
                        mm = pe.matmul(banks[:, 2 * (j % 2) + c_ // 2, (c_ % 2) * 256:(c_ % 2) * 256 + 256],
                                       e_ring[:, j % E_SLOTS, c_ * D:(c_ + 1) * D], W(f"ee{l}"), start=True, stop=True)
                    mm.then_inc(ve_mm.sem, 1)

                def add_squares(g, j):
                    wait(dve, (sq.sem, sq.n + g + 1))
                    wait(dve, (sq_add.sem, sq_add.n + g))
                    dve.tensor_tensor(sq_acc, sq_acc, sq_ring[:, j % 2, :], ALU.add).then_inc(sq_add.sem, 1)

                with nc.Fori(0, NG // UNROLL) as i:
                    relu_e(i, 0)
                    edge_product(i, 0)
                    for j in range(UNROLL):
                        g = i * UNROLL + j
                        load_idx(g, j, [src_g], st_mm)
                        load_e(g, j)
                        gather(i, j, [(tab2, 0, 2 * D)],
                               [(st_mm.sem, st_mm.n + g - (UNROLL - 1)), (sq.sem, sq.n + g - (UNROLL - 1)),
                                (pre_out[j].sem, pre_out[j].n + 16 * i)])
                        wait(dve, rows_ready(i, j))
                        wait(dve, (ve_mm.sem, ve_mm.n + g + 1))
                        p = m_ring[j].rearrange("p c f -> p (c f)")
                        v = banks[:, 2 * (j % 2):2 * (j % 2) + 2, :].rearrange("p b f -> p (b f)")
                        dve.tensor_tensor(p, p, v, ALU.add).then_inc(pre.sem, 1)
                        if j:
                            add_squares(g - 1, j - 1)
                        if j + 1 < UNROLL:
                            relu_e(i, j + 1)
                            edge_product(i, j + 1)
                        hold(act, (pre.sem, pre.n + g + 1))
                        act.dma_start(pre_dram[bass.ds(g, 1), :, :].rearrange("a p k -> (a p) k"), p
                                      ).then_inc(pre_out[j].sem, 16)
                        wait(act, (sq_add.sem, sq_add.n + g - 1))
                        act.activation(sq_ring[:, j % 2, :], p, ACT.Square).then_inc(sq.sem, 1)
                        wait(pe, (pre.sem, pre.n + g + 1))
                        for h in range(2):
                            mm = pe.matmul(st_ps[0:1, :], ones[:, 0:1], p[:, h * 512:(h + 1) * 512],
                                           start=False, stop=False, skip_group_check=True)
                        mm.then_inc(st_mm.sem, 1)
                    add_squares(g, j)
                rings_counted(idx=1, e=1, rows=1, pre_o=1)
                for q in (ve_mm, pre, sq, st_mm, sq_add) + ((e_relu,) if l else ()):
                    q.n += NG
                for k in range(4):
                    bank_free[k] = pre.now()

                wait(dve, st_mm.now())
                t = v_done.mark(dve.tensor_copy(sums_row[:, :], st_ps[0:1, :]))
                wait(dve, sq_add.now())
                for width in (4 * D, 2 * D):
                    t = v_done.mark(dve.tensor_tensor(sq_acc[:, 0:width], sq_acc[:, 0:width], sq_acc[:, width:2 * width],
                                                      ALU.add))
                    wait(dve, t)
                wait(pe, t)
                for h in range(2):
                    for k in range(2):
                        pe.matmul(x_ps[:, h:h + 1], sums_row[0:1, k * 256 + h * D:k * 256 + (h + 1) * D],
                                  ones[0:1, 0:1], start=(k == 0), stop=(k == 1))
                    mm = pe.matmul(x_ps[:, 2 + h:3 + h], sq_acc[:, h * D:(h + 1) * D], ones[:, 0:1],
                                   start=True, stop=True)
                t = p_done.mark(mm)

                wait(dve, t)
                v_done.mark(dve.tensor_scalar(MEAN, x_ps[:, 0:2], 1.0 / N_EDGES, None, ALU.mult))
                t = v_done.mark(dve.tensor_scalar(EX2, x_ps[:, 2:4], 1.0 / N_EDGES, None, ALU.mult))
                wait(dve, t)
                t = v_done.mark(dve.tensor_tensor(VAR, MEAN, MEAN, ALU.mult))
                wait(dve, t)
                t = v_done.mark(dve.tensor_tensor(VAR, EX2, VAR, ALU.subtract))
                wait(dve, t)
                t = v_done.mark(dve.tensor_scalar(VAR, VAR, 0.0, None, ALU.max))
                wait(act, t)
                t = a_done.mark(act.activation(S, VAR, ACT.Sqrt, bias=eps_c[:, :]))
                wait(dve, t)
                t = v_done.mark(dve.reciprocal(S, S))
                t = v_done.mark(dve.tensor_tensor(MEAN, MEAN, B1, ALU.add))
                wait(dve, t)
                t = v_done.mark(dve.tensor_tensor(SH, B1, MEAN, ALU.subtract))
                wait(dve, t)
                t = v_done.mark(dve.tensor_tensor(S, S, AB, ALU.mult))
                wait(dve, t)
                t = v_done.mark(dve.reciprocal(LOW, S))
                wait(dve, t)
                t = v_done.mark(dve.tensor_tensor(LOW, LOW, bet, ALU.mult))
                wait(dve, t)
                t = v_done.mark(dve.tensor_tensor(LOW, LOW, SH, ALU.add))
                wait(dve, t)
                t = v_done.mark(dve.tensor_scalar(LOW, LOW, -1.0, None, ALU.mult))
                v_done.mark(dve.tensor_tensor(SH, SH, S, ALU.mult))
                wait(dve, v_done.now())
                v_done.mark(dve.tensor_tensor(SH, SH, bet, ALU.add))
                t = spread(LOW, low, v_done.now())

                wait(dve, t, v_done.mark(dve.memset(sq_acc, 0.0)))
                wait(sp, *[q.now() for q in pre_out], st_mm.now(), sq.now(), sc_mm.now())
                sums = [(acc[:, 0, :], D), (acc[:, 1, :], D)]

                start_windows()
                with nc.Fori(0, NG // UNROLL) as i:
                    for j in range(UNROLL):
                        g = i * UNROLL + j
                        p = m_ring[j]
                        hold(sp, (sc_mm.sem, sc_mm.n + g - (UNROLL - 1)))
                        sp.dma_start(p.rearrange("p c f -> p (c f)"),
                                     pre_dram[bass.ds(g, 1), :, :].rearrange("a p k -> (a p) k")
                                     ).then_inc(pre_in[j].sem, 16)
                        wait(dve, (pre_in[j].sem, pre_in[j].n + 16 * (i + 1)))
                        dve.tensor_tensor(p, p, low[:, :].unsqueeze(1).to_broadcast([D, GC, 2 * D]), ALU.max
                                          ).then_inc(msg.sem, 1)
                        w0 = window_start(g - LAG)
                        wide_add(g, sums)
                        one_hot(g, j)
                        add_window(g, w0, j % 2, 2)
                        wait(pe, (msg.sem, msg.n + g + 1))
                        wide_mm(g, [(lambda c_, j=j: m_ring[j][:, c_, 0:D], D),
                                    (lambda c_, j=j: m_ring[j][:, c_, D:2 * D], D)])
                        window_mm(g, j, 2)
                        transpose_window(g, (j + 1) % 2, 2)
                        window_out(g, (j + 1) % 2, 2)
                finish_windows(2)
                rings_counted(pre_i=1)
                msg.n += NG

                for k in range(4):
                    bank_free[k] = sc_add.now()

                wait(pe, v_done.now(), sc_add.now())
                pe.matmul(x_ps[0:1, 0:D], SH[:, 0:1], W(f"eo_lo{l}"), start=True, stop=False)
                t = p_done.mark(pe.matmul(x_ps[0:1, 0:D], SH[:, 1:2], W(f"eo_hi{l}"), start=False, stop=True))
                wait(dve, t)
                v_done.mark(dve.tensor_tensor(v_row[:, :], x_ps[0:1, 0:D], row(f"eo_b{l}")[0:1, :], ALU.add))
                v_done.mark(dve.tensor_scalar(W(f"eo_lo{l}"), W(f"eo_lo{l}"), S[:, 0:1], None, ALU.mult))
                t = v_done.mark(dve.tensor_scalar(W(f"eo_hi{l}"), W(f"eo_hi{l}"), S[:, 1:2], None, ALU.mult))
                func = ACT.Relu if l < N_LAYERS2 - 1 else ACT.Identity
                t = product_T([(W(f"eo_lo{l}"), acc[:, 0, :]), (W(f"eo_hi{l}"), acc[:, 1, :]), (v_row[:, :], deg)],
                              [t, sc_add.now()], to_act(tA, func, 0.0))
                hT, h_ready = tA, [t]
                wait(dve, t)
            xn = add_and_norm(tA, h_ready)
            return xn

        def block3(xn_ready):
            src3, m = xN[:, :, :], [xn_ready]
            for layer, (w, b) in enumerate((("sage1", "sage_b1"), ("sage2", "sage_b2"))):
                s = sum_neighbours_again(src3, m)
                t = product_T([(W(w), acc[:, 0, :])], [s], to_act(tA, ACT.Relu, col(b)))
                if layer == 0:
                    m = T_to_N_wide(tA, [t])
                    src3 = tN[:, :, 0:D]
            return add_and_norm(tA, [t])

        xn_ready, xt_ready = block1(xn_ready, xt_ready)
        xn_ready = block2(xn_ready, xt_ready)
        xn_ready = block3(xn_ready)

        wait(sp, xn_ready)
        full = N_NODES // D
        out_w.mark(sp.dma_start(out[0:full * D, :].rearrange("(t p) f -> p t f", p=D), xN[:, 0:full, :]))
        out_w.mark(sp.dma_start(out[full * D:N_NODES, :], xN[0:N_NODES - full * D, full, :]))
        wait(sp, out_w.now(), table_w.now(), adj_st.now(), *[q.now() for q in pre_out])


WIDE_FROM = WIN


def kernel(**inputs):
    import numpy as np
    import concourse.bacc as bacc
    from concourse.bass_utils import run_bass_kernel_spmd

    a = {k: np.asarray(v) for k, v in inputs.items()}

    def padded(v, shape, fill):
        o = np.full(shape, fill, v.dtype)
        o[tuple(slice(0, n) for n in v.shape)] = v
        return o

    x = padded(a["x"], (NP, D), 0)
    src = padded(a["src"], (EP,), NP - 1).reshape(NG, GC, D)
    dst = padded(a["dst"], (EP,), -1).reshape(NG, GC, D)
    dst_ok = padded(a["dst"], (EP,), NP - 1).reshape(NG, GC, D)
    w = {"w1a": a["L0_gnn_w1a"], "w1b": a["L0_gnn_w1b"], "w2a": a["L0_gnn_w2a"], "w2b": a["L0_gnn_w2b"],
         "msg_xs": a["L1_gnn_msg_W1"][0:D], "msg_xd": a["L1_gnn_msg_W1"][D:2 * D], "msg_e": a["L1_gnn_msg_W1"][2 * D:],
         "msg_2": a["L1_gnn_msg_W2"], "upd_x": a["L1_gnn_upd_W1"][0:D], "upd_a": a["L1_gnn_upd_W1"][D:],
         "upd_2": a["L1_gnn_upd_W2"], "sage1": a["L3_gnn_W1"].T, "sage2": a["L3_gnn_W2"].T}
    c = {"b1a": a["L0_gnn_b1a"], "g1": a["L0_gnn_g1"], "bt1": a["L0_gnn_bt1"], "b1b": a["L0_gnn_b1b"],
         "b2a": a["L0_gnn_b2a"], "g2": a["L0_gnn_g2"], "bt2": a["L0_gnn_bt2"], "b2b": a["L0_gnn_b2b"],
         "upd_b1": a["L1_gnn_upd_b1"], "upd_b2": a["L1_gnn_upd_b2"], "sage_b1": a["L3_gnn_b1"], "sage_b2": a["L3_gnn_b2"]}
    r = {"msg_b1": a["L1_gnn_msg_b1"], "msg_b2": a["L1_gnn_msg_b2"], "ln_g": a["L1_gnn_ln_gamma"],
         "ln_b": a["L1_gnn_ln_beta"]}
    for l in range(N_LAYERS2):
        w1, w2 = a["L2_gnn_W1"][l].T, a["L2_gnn_W2"][l].T
        w |= {f"eh{l}": w1[0:D], f"ee{l}": w1[D:], f"eo_lo{l}": w2[0:D], f"eo_hi{l}": w2[D:]}
        for h in range(2):
            part = slice(h * D, (h + 1) * D)
            c |= {f"b{l}{h}": a["L2_gnn_b1"][l][part], f"g{l}{h}": a["L2_gnn_gamma"][l][part],
                  f"bt{l}{h}": a["L2_gnn_beta"][l][part]}
        r[f"eo_b{l}"] = a["L2_gnn_b2"][l]
    arrays = {
        "x_n": x, "x_t": x.T, "e_t": padded(a["edge_attr_128"], (EP, D), 0).T,
        "src_g": src.transpose(0, 2, 1), "dst_g": dst_ok.transpose(0, 2, 1),
        "dst_p": dst.reshape(NG * GC, D).T, "dst_row": dst.reshape(NG, GE),
        "src_p": src.reshape(NG * GC, D).T,
        "weights": np.concatenate([w[k] for k in WEIGHTS], axis=1),
        "cols": np.stack([c[k] for k in COLS], axis=1), "rows": np.stack([r[k] for k in ROWS]),
        "eps": np.stack([a["L0_gnn_eps1"], a["L0_gnn_eps2"]]).reshape(1, 2),
    }
    arrays = {k: np.ascontiguousarray(v) for k, v in arrays.items()}
    nc = bacc.Bacc("TRN2", target_bir_lowering=False, num_devices=1)
    args = [nc.dram_tensor(k, v.shape, mybir.dt.from_np(v.dtype), kind="ExternalInput").ap() for k, v in arrays.items()]
    o = nc.dram_tensor("out", (N_NODES, D), F32, kind="ExternalOutput").ap()
    build(nc, *args, o)
    return run_bass_kernel_spmd(nc, [arrays], core_ids=[0]).results[0]["out"]
```
